# Optimizing a Trainium2 kernel written in Bass

```python
import numpy as np
import jax
import jax.numpy as jnp

def _softmax(x, axis=-1):
    return jax.nn.softmax(x, axis=axis)

def _gelu(x):
    return jax.nn.gelu(x, approximate=True)

def _silu(x):
    return jax.nn.silu(x)

def _sigmoid(x):
    return jax.nn.sigmoid(x)

def _layernorm(x, axis=-1, eps=1e-05):
    m = jnp.mean(x, axis=axis, keepdims=True)
    v = jnp.var(x, axis=axis, keepdims=True)
    return (x - m) / jnp.sqrt(v + eps)

def _scatter_add(tgt, idx, src, axis=0):
    return tgt.at[idx].add(src)

def _segment_sum(src, seg, n):
    return jax.ops.segment_sum(src, seg, n)
kernel_name = 'mk_decoder_preln_d1_seqx_r4_60fcab'

def setup_inputs(seed: int=0):
    np.random.seed(seed)
    _w = jnp.asarray

    def _rec_inputs():
        import jax
        import jax.numpy as jnp
        _rk = jax.random.key(seed)
        x = -0.0002928 + 1 * jax.random.normal(jax.random.fold_in(_rk, 1), (2, 1024, 256), jnp.float32)
        _lenS = 1024 - jax.random.randint(jax.random.fold_in(_rk, 7), (2,), 0, max(1, 1024 // 4) + 1, jnp.int32)
        _lenS2 = 77 - jax.random.randint(jax.random.fold_in(_rk, 8), (2,), 0, max(1, 77 // 4) + 1, jnp.int32)
        _ctx_768P = jax.random.normal(jax.random.fold_in(_rk, 11), (2, 16, 192), jnp.float32)
        _ctx_768c = jax.random.dirichlet(jax.random.fold_in(_rk, 511), 0.3 * jnp.ones((16,), jnp.float32), (2, 77))
        _ctx_768t = jnp.einsum('bsk,bkd->bsd', _ctx_768c, _ctx_768P)
        _ctx_768t = _ctx_768t * jax.lax.rsqrt(jnp.mean(jnp.square(_ctx_768t)) + 1e-12) * 0.953939
        ctx_768 = 2.09791e-05 + 1.00001 * (_ctx_768t + 0.3 * jax.random.normal(jax.random.fold_in(_rk, 611), (2, 77, 192), jnp.float32))
        return (x, ctx_768)
    x, ctx_768 = _rec_inputs()

    def _L0_attn_setup():
        import jax, jax.numpy as jnp
        import numpy as np
        B, L, D, H, W = (2, 256, 256, 16, 64)
        DH = D // H
        key = jax.random.key(seed)
        ks = jax.random.split(key, 7)
        scale = 0.02
        return {'x': jax.random.normal(ks[0], (B, L, D), dtype=jnp.float32), 'Wq': jax.random.normal(ks[1], (D, D), dtype=jnp.float32) * scale, 'Wk': jax.random.normal(ks[2], (D, D), dtype=jnp.float32) * scale, 'Wv': jax.random.normal(ks[3], (D, D), dtype=jnp.float32) * scale, 'Wo': jax.random.normal(ks[4], (D, D), dtype=jnp.float32) * scale, 'last_k_init': jax.random.normal(ks[5], (W - 1, H, DH), dtype=jnp.float32), 'last_v_init': jax.random.normal(ks[6], (W - 1, H, DH), dtype=jnp.float32)}
    _L0_attn_all = _L0_attn_setup()
    _L0_attn_in = {k: v for k, v in _L0_attn_all.items() if k in ('Wq', 'Wk', 'Wv', 'Wo', 'last_k_init', 'last_v_init')}
    del _L0_attn_all

    def _L0_xattn_setup():
        import jax, jax.numpy as jnp
        import numpy as np
        N_HEADS = 16
        D_HEAD = 64
        key = jax.random.key(seed)
        ks = jax.random.split(key, 7)
        B, SQ, SKV = (2, 512, 512)
        D_MODEL, D_COND, D_ATTN = (256, 192, N_HEADS * D_HEAD)
        return {'x': jax.random.normal(ks[0], (B, SQ, D_MODEL), jnp.float32), 'cond': jax.random.normal(ks[1], (B, SKV, D_COND), jnp.float32), 'w_q': jax.random.normal(ks[2], (D_MODEL, D_ATTN), jnp.float32) * D_MODEL ** (-0.5), 'w_k': jax.random.normal(ks[3], (D_COND, D_ATTN), jnp.float32) * D_COND ** (-0.5), 'w_v': jax.random.normal(ks[4], (D_COND, D_ATTN), jnp.float32) * D_COND ** (-0.5), 'w_out': jax.random.normal(ks[5], (D_ATTN, D_MODEL), jnp.float32) * D_ATTN ** (-0.5), 'b_out': jnp.zeros((D_MODEL,), jnp.float32)}
    _L0_xattn_all = _L0_xattn_setup()
    _L0_xattn_in = {k: v for k, v in _L0_xattn_all.items() if k in ('w_q', 'w_k', 'w_v', 'w_out', 'b_out')}
    del _L0_xattn_all

    def _L0_ffn_setup():
        import jax, jax.numpy as jnp
        import numpy as np
        D_MODEL = 256
        D_FF = 1024
        N_EXP = 8
        TOP_K = 2

        def _gelu(x):
            return jax.nn.gelu(x, approximate=False)
        key = jax.random.key(seed)
        ks = jax.random.split(key, 12)
        s = 0.02
        return {'x': jax.random.normal(ks[0], (4, 512, D_MODEL), dtype=jnp.float32), 'shared_w1': jax.random.normal(ks[1], (D_MODEL, D_FF), dtype=jnp.float32) * s, 'shared_b1': jnp.zeros((D_FF,), jnp.float32), 'shared_w2': jax.random.normal(ks[2], (D_FF, D_MODEL), dtype=jnp.float32) * s, 'shared_b2': jnp.zeros((D_MODEL,), jnp.float32), 'router_w': jax.random.normal(ks[3], (D_MODEL, N_EXP), dtype=jnp.float32) * s, 'router_b': jnp.zeros((N_EXP,), jnp.float32), 'exp_w1': jax.random.normal(ks[4], (N_EXP, D_MODEL, D_FF), dtype=jnp.float32) * s, 'exp_b1': jnp.zeros((N_EXP, D_FF), jnp.float32), 'exp_w2': jax.random.normal(ks[5], (N_EXP, D_FF, D_MODEL), dtype=jnp.float32) * s, 'exp_b2': jnp.zeros((N_EXP, D_MODEL), jnp.float32)}
    _L0_ffn_all = _L0_ffn_setup()
    _L0_ffn_in = {k: v for k, v in _L0_ffn_all.items() if k in ('shared_w1', 'shared_b1', 'shared_w2', 'shared_b2', 'router_w', 'router_b', 'exp_w1', 'exp_b1', 'exp_w2', 'exp_b2')}
    del _L0_ffn_all
    return {'x': x, 'ctx_768': ctx_768, 'L0_attn_Wq': _L0_attn_in['Wq'], 'L0_attn_Wk': _L0_attn_in['Wk'], 'L0_attn_Wv': _L0_attn_in['Wv'], 'L0_attn_Wo': _L0_attn_in['Wo'], 'L0_attn_last_k_init': _L0_attn_in['last_k_init'], 'L0_attn_last_v_init': _L0_attn_in['last_v_init'], 'L0_xattn_w_q': _L0_xattn_in['w_q'], 'L0_xattn_w_k': _L0_xattn_in['w_k'], 'L0_xattn_w_v': _L0_xattn_in['w_v'], 'L0_xattn_w_out': _L0_xattn_in['w_out'], 'L0_xattn_b_out': _L0_xattn_in['b_out'], 'L0_ffn_shared_w1': _L0_ffn_in['shared_w1'], 'L0_ffn_shared_b1': _L0_ffn_in['shared_b1'], 'L0_ffn_shared_w2': _L0_ffn_in['shared_w2'], 'L0_ffn_shared_b2': _L0_ffn_in['shared_b2'], 'L0_ffn_router_w': _L0_ffn_in['router_w'], 'L0_ffn_router_b': _L0_ffn_in['router_b'], 'L0_ffn_exp_w1': _L0_ffn_in['exp_w1'], 'L0_ffn_exp_b1': _L0_ffn_in['exp_b1'], 'L0_ffn_exp_w2': _L0_ffn_in['exp_w2'], 'L0_ffn_exp_b2': _L0_ffn_in['exp_b2']}

def reference(x, ctx_768, L0_attn_Wq, L0_attn_Wk, L0_attn_Wv, L0_attn_Wo, L0_attn_last_k_init, L0_attn_last_v_init, L0_xattn_w_q, L0_xattn_w_k, L0_xattn_w_v, L0_xattn_w_out, L0_xattn_b_out, L0_ffn_shared_w1, L0_ffn_shared_b1, L0_ffn_shared_w2, L0_ffn_shared_b2, L0_ffn_router_w, L0_ffn_router_b, L0_ffn_exp_w1, L0_ffn_exp_b1, L0_ffn_exp_w2, L0_ffn_exp_b2):
    import jax
    import jax.numpy as jnp

    def _L0_attn_ref(x, Wq, Wk, Wv, Wo, last_k_init, last_v_init):
        import jax, jax.numpy as jnp
        import numpy as np
        B, L, D, H, W = (2, 256, 256, 16, 64)
        DH = D // H
        b, l, d = x.shape
        w1, h, dh = last_k_init.shape
        w = w1 + 1
        q = (x @ Wq.T).reshape(b, l, h, dh)
        k = (x @ Wk.T).reshape(b, l, h, dh)
        v = (x @ Wv.T).reshape(b, l, h, dh)
        last_k = jnp.broadcast_to(last_k_init[None], (b, w1, h, dh))
        last_v = jnp.broadcast_to(last_v_init[None], (b, w1, h, dh))
        k_pad = jnp.concatenate([last_k, k], axis=1)
        v_pad = jnp.concatenate([last_v, v], axis=1)
        idx = jnp.arange(l)[:, None] + jnp.arange(w)[None, :]
        k_win = k_pad[:, idx]
        v_win = v_pad[:, idx]
        scores = jnp.einsum('blhd,blwhd->blwh', q, k_win) * dh ** (-0.5)
        attn = jax.nn.softmax(scores, axis=2)
        out = jnp.einsum('blwh,blwhd->blhd', attn, v_win).reshape(b, l, d)
        return out @ Wo.T

    def _L0_xattn_ref(x, cond, w_q, w_k, w_v, w_out, b_out):
        import jax, jax.numpy as jnp
        import numpy as np
        N_HEADS = 16
        D_HEAD = 64
        B, SQ, _ = x.shape
        SKV = cond.shape[1]
        scale = D_HEAD ** (-0.5)
        q = (x @ w_q).reshape(B, SQ, N_HEADS, D_HEAD)
        k = (cond @ w_k).reshape(B, SKV, N_HEADS, D_HEAD)
        v = (cond @ w_v).reshape(B, SKV, N_HEADS, D_HEAD)
        attn = jnp.einsum('bqhd,bkhd->bhqk', q, k) * scale
        attn = jax.nn.softmax(attn, axis=-1)
        out = jnp.einsum('bhqk,bkhd->bqhd', attn, v).reshape(B, SQ, N_HEADS * D_HEAD)
        return out @ w_out + b_out

    def _L0_ffn_ref(x, shared_w1, shared_b1, shared_w2, shared_b2, router_w, router_b, exp_w1, exp_b1, exp_w2, exp_b2):
        import jax, jax.numpy as jnp
        import numpy as np
        D_MODEL = 256
        D_FF = 1024
        N_EXP = 8
        TOP_K = 2

        def _gelu(x):
            return jax.nn.gelu(x, approximate=False)
        leading = x.shape[:-1]
        d = x.shape[-1]
        xf = x.reshape(-1, d)
        T = xf.shape[0]
        h_shared = _gelu(xf @ shared_w1 + shared_b1) @ shared_w2 + shared_b2
        logits = xf @ router_w + router_b
        routing = jax.nn.softmax(logits, axis=-1)
        sel_w, sel_idx = jax.lax.top_k(routing, TOP_K)
        sel_w = sel_w / (jnp.sum(sel_w, axis=-1, keepdims=True) + 1e-09)
        combine = jnp.zeros((T, N_EXP), routing.dtype)
        combine = combine.at[jnp.arange(T)[:, None], sel_idx].add(sel_w)
        residual = jnp.zeros_like(xf)
        for e in range(N_EXP):
            h = _gelu(xf @ exp_w1[e] + exp_b1[e])
            y = h @ exp_w2[e] + exp_b2[e]
            residual = residual + combine[:, e:e + 1] * y
        out = h_shared + residual
        return out.reshape(*leading, d)
    x = x + _L0_attn_ref(_layernorm(x, axis=-1), L0_attn_Wq, L0_attn_Wk, L0_attn_Wv, L0_attn_Wo, L0_attn_last_k_init, L0_attn_last_v_init)
    x = x + _L0_xattn_ref(_layernorm(x, axis=-1), ctx_768, L0_xattn_w_q, L0_xattn_w_k, L0_xattn_w_v, L0_xattn_w_out, L0_xattn_b_out)
    x = x + _L0_ffn_ref(_layernorm(x, axis=-1), L0_ffn_shared_w1, L0_ffn_shared_b1, L0_ffn_shared_w2, L0_ffn_shared_b2, L0_ffn_router_w, L0_ffn_router_b, L0_ffn_exp_w1, L0_ffn_exp_b1, L0_ffn_exp_w2, L0_ffn_exp_b2)
    return x

_drawn_inputs = setup_inputs


def setup_inputs(seed=0):
    import zlib

    import numpy as np

    out = dict(_drawn_inputs(seed))
    spreads = {'L0_xattn_b_out': (0.0, 0.1),
     'L0_ffn_shared_b1': (0.0, 0.292),
     'L0_ffn_shared_b2': (0.0, 0.1),
     'L0_ffn_router_b': (0.0, 0.291),
     'L0_ffn_exp_b1': (0.0, 0.369),
     'L0_ffn_exp_b2': (0.0, 0.1)}
    factors = {'L0_attn_Wq': 8.0,
     'L0_attn_Wk': 8.0,
     'L0_attn_Wv': 3.878,
     'L0_attn_Wo': 3.428,
     'L0_attn_last_k_init': 8.0,
     'L0_attn_last_v_init': 6.898}
    for name, (base, spread) in spreads.items():
        noise = np.random.default_rng([zlib.crc32(name.encode()), seed]).standard_normal(out[name].shape)
        drawn = base * np.exp(spread * noise) if base else spread * noise
        out[name] = jnp.asarray(drawn.astype(out[name].dtype))
    for name, factor in factors.items():
        out[name] = (out[name] * factor).astype(out[name].dtype)
    return out
```

```python
import numpy as np
import concourse.bass as bass
from concourse import mybir
from concourse.alu_op_type import AluOpType as ALU

ACT = mybir.ActivationFunctionType
AX = mybir.AxisListType
F32 = mybir.dt.float32
F32R = mybir.dt.float32r
BF16 = mybir.dt.bfloat16
I32 = mybir.dt.int32
U32 = mybir.dt.uint32

P = 128
EPS = 1e-5
MASKED = -1e30
CREDIT = 64


class Region:

    def __init__(self, nc, start, end):
        self.nc, self.at, self.end = nc, start, end

    def place(self, name, shape, dtype):
        size = int(np.prod(shape[1:])) * (2 if dtype == BF16 else 4)
        t = self.nc.alloc_sbuf_tensor_at(name, shape, dtype, offset=self.at)
        self.at += (size + 63) // 64 * 64
        assert self.at <= self.end, (name, self.at, self.end)
        return t


def sweep(eng, base, pairs, body, stages=3):
    lag = stages // 2 * 2
    for k in range(lag):
        body(base + k, k % 2, [n <= k for n in range(stages)])
    with eng.Fori(lag // 2, pairs) as j:
        body(base + j * 2, 0, [True] * stages)
        body(base + j * 2 + 1, 1, [True] * stages)
    for k in range(stages - 1):
        body(base + pairs * 2 + k, k % 2, [n > k for n in range(stages)])


def decoder_layer(nc, x, ctx, wq, wk, wv, wo, last_k, last_v, xq, xk, xv, xo, xb,
                  sw1, sb1, sw2, sb2, rw, rb, ew1, eb1, ew2, eb2, out):
    B, L, D = x.shape
    TOK = B * L
    NT = TOK // P
    TB = L // P
    W1, H, DH = last_k.shape
    W = W1 + 1
    DC = D // P
    CK, CD = ctx.shape[1:]
    XA = xq.shape[1]
    XH = 16
    XD = XA // XH
    HP = XA // P
    FL = XH * CK
    FC = -(-FL // P)
    FLAST = FL - (FC - 1) * P
    E, _, FF = ew1.shape
    KF = FF // P
    BLOCKS = (2 * TOK) // P + E
    VROW = DH + 1
    KW = P + W

    b1_rows = nc.dram_tensor("b1_rows", [3, E + 1, FF], BF16, kind="Internal").ap()
    b2_rows = nc.dram_tensor("b2_rows", [3, E + 2, D], BF16, kind="Internal").ap()
    slot_x = nc.dram_tensor("slot_x", [BLOCKS * P, D], F32, kind="Internal").ap()
    slot_y = nc.dram_tensor("slot_y", [BLOCKS * P, D], F32, kind="Internal").ap()

    xf = x.rearrange("b l d -> (b l) d").rearrange("(t p) d -> p t d", p=P)
    of = out.rearrange("b l d -> (b l) d").rearrange("(t p) d -> p t d", p=P)

    base = (nc.sbuf_base + 63) // 64 * 64
    top = nc.sbuf_usable_end
    keep = Region(nc, base, base + 24 * 1024)
    X = keep.place("X", [P, NT, D], F32)
    ident = keep.place("ident", [P, P], F32)
    identb = keep.place("identb", [P, P], BF16)
    window = keep.place("window", [P, 2 * KW], BF16)
    ones = keep.place("ones", [P, P], F32)
    onesb = keep.place("onesb", [P, P], BF16)
    before = keep.place("before", [P, P], F32)
    rw_sb = keep.place("rw_sb", [P, DC, E], F32)
    rb_sb = keep.place("rb_sb", [1, E], F32)
    minus_half = keep.place("minus_half", [P, 1], F32)
    b_out = keep.place("b_out", [P, D], F32)

    r1 = keep.at
    R1 = 48 * 1024
    r2 = r1 + R1
    R2 = 81 * 1024
    r3 = r2 + R2

    WN = 2 * KF * D
    reg = Region(nc, r1, r3)
    raw = reg.place("raw", [P, WN], F32)
    wts = reg.place("wts", [P, 2, 2, WN], F32R)
    after_wts = reg.at

    reg = Region(nc, r2, r3)
    Ah = reg.place("Ah", [P, B, DC, FL], F32R)
    Al = reg.place("Al", [P, B, DC, FL], F32R)
    VWh = reg.place("VWh", [P, B, FC, D], F32R)
    VWl = reg.place("VWl", [P, B, FC, D], F32R)

    reg = Region(nc, r3, top)
    WTh = reg.place("WTh", [P, DC, 4 * D], F32R)
    WTl = reg.place("WTl", [P, DC, 4 * D], F32R)
    kinit = reg.place("kinit", [P, H // 2, W], F32R)
    vinit = reg.place("vinit", [P, H, VROW], F32)
    qs = reg.place("qs", [P, H, 64], F32)
    ks = reg.place("ks", [P, H, 64], F32)
    r3b = reg.at
    xn = reg.place("xn", [P, D], F32)
    xth = reg.place("xth", [P, DC, P], F32R)
    xtl = reg.place("xtl", [P, DC, P], F32R)
    stats = reg.place("stats", [P, 16], F32)
    idle = Region(nc, r1 + 4 * WN, r2)
    qe = [idle.place(f"qe{i}", [P, H // 2, P], F32R) for i in range(2)]
    qo = [idle.place(f"qo{i}", [P, H // 2, P], F32R) for i in range(2)]
    kst = [reg.place(f"kst{i}", [P, H // 2, P], F32R) for i in range(2)]
    V = [reg.place(f"V{i}", [P, H, VROW], F32) for i in range(2)]
    vprev = [reg.place(f"vprev{i}", [P, H, VROW], F32) for i in range(2)]
    negm = reg.place("negm", [P, 2, H], F32)
    prob = [reg.place(f"prob{i}", [P, 2 * KW], F32) for i in range(2)]
    pt = [reg.place(f"pt{i}", [P, 3, P], F32) for i in range(2)]
    rden = reg.place("rden", [P, H], F32)
    o_sb = reg.place("o_sb", [P, D], F32)
    oth = reg.place("oth", [P, DC, P], F32R)
    otl = reg.place("otl", [P, DC, P], F32R)

    reg = Region(nc, r1, r2)
    wqT = reg.place("wqT", [P, HP, D], F32)
    xo_sb = reg.place("xo_sb", [P, HP, D], F32)
    KB = reg.place("KB", [P, B, HP, 2 * CK], F32)
    xk_sb = reg.place("xk_sb", [P, 2, XA], F32)
    cT = reg.place("cT", [P, 2, B * CK], F32)
    ctx_sb = reg.place("ctx_sb", [CK, B, CD], F32)
    lastk = reg.place("lastk", [W, H, DH], F32)
    reg = Region(nc, r3b, top)
    VZ = P + 2 * CK + P
    VB = reg.place("VB", [P, HP, B, VZ], F32)
    reg = Region(nc, r2, r3)
    xv_sb = reg.place("xv_sb", [P, 2, XA], F32)
    w4 = reg.place("w4", [P, 4, DC, D], F32)
    xq_sb = reg.place("xq_sb", [P, DC, XA], F32)
    reg = Region(nc, r2 + 2 * 4 * B * DC * FL + 4 * B * FC * D, r3)
    bias1 = reg.place("bias1", [E + 1, FF], F32)
    bias1p = reg.place("bias1p", [E + 1, 3, FF], BF16)
    bias2 = reg.place("bias2", [E + 2, D], F32)
    bias2p = reg.place("bias2p", [E + 2, 3, D], BF16)

    reg = Region(nc, r3, top)
    XN3 = reg.place("XN3", [P, NT, D], F32)
    r3c = reg.at
    logits = reg.place("logits", [P, NT, E], F32)
    XN3c = reg.place("XN3c", [P, D], F32)
    xn2 = reg.place("xn2", [P, D], F32)
    xt2h = reg.place("xt2h", [P, DC, P], F32R)
    xt2l = reg.place("xt2l", [P, DC, P], F32R)
    negm2 = reg.place("negm2", [P, XH], F32)
    den2 = reg.place("den2", [P, 2, XH], F32)
    prob2 = [reg.place(f"prob2_{i}", [P, XH, CK], F32) for i in range(2)]
    pth = reg.place("pth", [P, FC, P], F32R)
    ptl = reg.place("ptl", [P, FC, P], F32R)
    x3t = reg.place("x3t", [P, DC, P], F32)
    stats2 = reg.place("stats2", [P, 16], F32)

    reg = Region(nc, after_wts, r3)
    b1r = reg.place("b1r", [3, (E + 1) * FF], BF16)
    reg = Region(nc, r3c + NT * E * 4, top)
    b2r = reg.place("b2r", [3, (E + 2) * D], BF16)
    xf_sb = [reg.place(f"xf{i}", [P, D], F32) for i in range(2)]
    fxh = reg.place("fxh", [P, DC, P], F32R)
    fxl = reg.place("fxl", [P, DC, P], F32R)
    hact = reg.place("hact", [P, FF], F32)
    hth = reg.place("hth", [P, KF, P], F32R)
    htl = reg.place("htl", [P, KF, P], F32R)
    y_sb = [reg.place(f"y{i}", [P, D], F32) for i in range(2)]
    e8 = [reg.place(f"e8_{i}", [P, NT, E], F32) for i in range(6)]
    s16 = [reg.place(f"s16_{i}", [P, NT], F32) for i in range(4)]
    run = [reg.place(f"run{i}", [P, NT, E], F32) for i in range(3)]
    pairs_i = reg.place("pairs_i", [1, 1], I32)
    best = reg.place("best", [P, NT, 8], F32)
    besti = reg.place("besti", [P, NT, 8], U32)
    bestf = reg.place("bestf", [P, NT, 2], F32)
    gate = reg.place("gate", [P, NT, 2], F32)
    destf = reg.place("destf", [P, 2, NT], F32)
    dest = reg.place("dest", [P, 2, NT], I32)
    iota8 = reg.place("iota8", [P, E], F32)
    iotab = reg.place("iotab", [1, BLOCKS], F32)
    counts = [reg.place(f"counts{i}", [P, E], F32) for i in range(4)]
    countsi = [reg.place(f"countsi{i}", [P, E], I32) for i in range(2)]
    owner8 = reg.place("owner8", [1, BLOCKS, E], F32)
    owner = [reg.place(f"owner{i}", [1, BLOCKS], F32) for i in range(2)]
    stage_of = reg.place("stage_of", [1, BLOCKS], I32)
    place_of = reg.place("place_of", [1, BLOCKS], I32)
    ends = reg.place("ends", [1, E + 1], I32)
    zeros = reg.place("zeros", [P, D], F32)
    ya = [reg.place(f"ya{i}", [P, D], F32) for i in range(2)]
    yb = [reg.place(f"yb{i}", [P, D], F32) for i in range(2)]

    PQ = [nc.alloc_psum_tensor(f"PQ{i}", [P, 2, 512], F32) for i in range(4)]

    RT_SHIFTED, RT_SEL = 2, 10
    sel = e8[4][:, :, :]
    rank_ps, total_ps = PQ[0][:, 0, 0:NT * E], PQ[0][:, 1, 0:NT * E]
    run0 = run[2][:, :, :]

    sems = {}

    def sem(name):
        sems[name] = nc.alloc_semaphore(name)
        return sems[name]

    def split_product(pe, o, left, right, start, stop):
        (lh, ll), (rh, rl) = left, right
        pe.matmul(o, lh, rh, start=start, stop=False)
        pe.matmul(o, lh, rl, start=False, stop=False)
        return pe.matmul(o, ll, rh, start=False, stop=stop)

    passed = sem("passed")

    def pass_waits(eng):
        eng.sem_inc(passed, 1)

    ld = {n: sem("ld_" + n) for n in ("x", "w4", "ctx", "last", "lastv", "xq", "xk", "xv", "xo", "bias",
                                      "small", "brow", "b1r")}
    made = sem("made")
    made_steps = sem("made_steps")
    p_pe, p_act, p_dve = sem("p_pe"), sem("p_act"), sem("p_dve")
    p_steps = sem("p_steps")
    bias_split = sem("bias_split")
    ks_hi, ks_lo, ks_dup = sem("ks_hi"), sem("ks_lo"), sem("ks_dup")
    a_names = ("ln", "xn", "xT", "xh", "xl", "qkv", "hi", "lo", "dup", "v", "qT", "qE", "qO", "kT",
               "kA", "kD", "S", "max", "exp", "tr", "ev0", "ev1", "pv", "rd", "on", "oT", "oh",
               "ol", "op", "x1")
    a = {n: sem("a_" + n) for n in a_names}
    a_vp = [sem("a_vp0"), sem("a_vp1")]
    a_k0 = sem("a_k0")
    c_names = ("ln", "xn", "xT", "xh", "xl", "S", "max", "exp", "rd", "nrm", "pT", "ph", "pl", "o",
               "x2", "bo", "ln3", "xn3", "x3c", "x3T", "x3", "lg", "lgc")
    c = {n: sem("c_" + n) for n in c_names}
    rt, rt_act, rt_pe, rt_idx, rt_done = (sem(n) for n in ("rt", "rt_act", "rt_pe", "rt_idx", "rt_done"))
    ld_raw, ld_raw_pool, w_split = sem("ld_raw"), sem("ld_raw_pool"), sem("w_split")
    zeroed, scattered, z_made = sem("zeroed"), sem("scattered"), sem("z_made")
    f_names = ("xT", "xh", "xl", "up", "act", "hT", "hh", "hl", "dn", "y")
    f = {n: sem("f_" + n) for n in f_names}
    f_x = [sem("f_x0"), sem("f_x1")]
    f_st = [sem("f_st0"), sem("f_st1")]
    g_y = [sem("g_y0"), sem("g_y1")]
    g_add, g_done, g_mid = sem("g_add"), sem("g_done"), sem("g_mid")
    credited = [*a.values(), *c.values(), *f.values(), *a_vp, *f_st]
    C = CREDIT

    block_ctx = nc.Block()
    block = block_ctx.__enter__()

    CH_WT, CH_CT, CH_KI, CH_WQ, CH_K, CH_V, CH_A, CH_VW = 0, 2, 3, 4, 6, 8, 10, 18
    CHUNKS = 24
    HALF = FL // 2
    VW_CH = [(b, n) for b in range(B) for n in range(0, FC, 4)]

    def vw_rows(n):
        return P if n < FC - 1 else FLAST

    @block.sync
    def _(sp):
        for n, w in enumerate((wq, wk, wv, wo)):
            sp.dma_start(w4[:, n, :, :], w.rearrange("(c p) i -> p c i", p=P)).then_inc(ld["w4"], 16)
        sp.wait_ge(made_steps, 9)
        sp.dma_start(lastk[1:W, :, :], last_k).then_inc(ld["last"], 16)
        sp.dma_start(ctx_sb[:, :, :], ctx.rearrange("b k d -> k b d")).then_inc(ld["ctx"], 16)
        sp.dma_start(xq_sb[:, :, :], xq.rearrange("(c p) n -> p c n", p=P)).then_inc(ld["xq"], 16)
        for t, w, s in ((xk_sb, xk, "xk"), (xv_sb, xv, "xv")):
            sp.dma_start(t[:, 0, :], w[0:P, :]).then_inc(ld[s], 16)
            sp.dma_start(t[0:CD - P, 1, :], w[P:CD, :]).then_inc(ld[s], 16)
        sp.dma_start(xo_sb[:, :, :], xo.rearrange("(c p) n -> p c n", p=P)).then_inc(ld["xo"], 16)
        sp.dma_start(X[:, :, :], xf).then_inc(ld["x"], 16)
        sp.wait_ge(bias_split, 6)
        for r in range(3):
            sp.dma_start(b1_rows[r], bias1p[:, r, :]).then_inc(ld["brow"], 16)
            sp.dma_start(b2_rows[r], bias2p[:, r, :]).then_inc(ld["brow"], 16)
        sp.wait_ge(p_pe, CHUNKS)
        sp.dma_start(raw[:, 0:DC * FF].rearrange("p (c f) -> p c f", c=DC),
                     sw1.rearrange("(c p) f -> p c f", p=P)).then_inc(ld_raw, 16)
        sp.dma_start(raw[:, DC * FF:].rearrange("p (c n) -> p c n", c=KF),
                     sw2.rearrange("(c p) n -> p c n", p=P)).then_inc(ld_raw, 16)

        def prev_values(t, k):
            sp.wait_ge(a["pv"], C + 8 * t - 8)
            pass_waits(sp)
            if k == 0:
                sp.wait_ge(made, 9)
                src = vinit[W:P, :, :]
            else:
                sp.wait_ge(a["v"], C + t)
                src = V[1 - k % 2][W:P, :, :]
            for n in range(2):
                half = vprev[k % 2][n * W:(n + 1) * W, :, :].rearrange("p (g n r) v -> p g n (r v)", n=2, r=2)[:, :, n, :]
                sp.dma_start(half, src.rearrange("p (g n r) v -> p g n (r v)", n=2, r=2)[:, :, n, :]).then_inc(a_vp[k % 2], 16)

        with sp.Fori(0, B) as b:
            prev_values(b * TB, 0)
            prev_values(b * TB + 1, 1)
            with sp.Fori(1, TB // 2) as j:
                prev_values(b * TB + j * 2, 2)
                prev_values(b * TB + j * 2 + 1, 3)

        sp.wait_ge(c["x2"], C + NT)
        sp.wait_ge(ld["brow"], 16 * 6)
        sp.dma_start(b1r[:, :], b1_rows.rearrange("r e f -> r (e f)")).then_inc(ld["b1r"], 16)
        sp.wait_ge(c["lgc"], C + NT)
        sp.dma_start(b2r[:, :], b2_rows.rearrange("r e f -> r (e f)")).then_inc(ld["b1r"], 16)
        sp.wait_ge(z_made, 1)
        slot_tiles = slot_x.rearrange("(t p) d -> t p d", p=P)
        with sp.Fori(0, BLOCKS) as t:
            sp.dma_start(slot_tiles[bass.ds(t, 1)].rearrange("t p d -> p (t d)"), zeros[:, :]).then_inc(zeroed, 16)
        slot_out = slot_y.rearrange("(t p) d -> t p d", p=P)
        with sp.Fori(2 * NT, BLOCKS) as t:
            sp.dma_start(slot_out[bass.ds(t, 1)].rearrange("t p d -> p (t d)"), zeros[:, :]).then_inc(zeroed, 16)

        def raw_weights(e):
            sp.wait_ge(w_split, 2 * (e + 1))
            sp.dma_start(raw[:, 0:DC * FF].rearrange("p (c f) -> p c f", c=DC),
                         ew1[e].rearrange("(c p) f -> p c f", p=P)).then_inc(ld_raw, 16)
            sp.dma_start(raw[:, DC * FF:].rearrange("p (c n) -> p c n", c=KF),
                         ew2[e].rearrange("(c p) n -> p c n", p=P)).then_inc(ld_raw, 16)

        raw_weights(0)
        raw_weights(1)

        def load_shared(i, par):
            sp.wait_ge(f["xT"], C + i - 1)
            sp.dma_start(xf_sb[par][:, :], XN3[:, bass.ds(i, 1), :].rearrange("p t d -> p (t d)")).then_inc(f_x[par], 16)

        sp.wait_ge(c["x3c"], C + NT)
        with sp.Fori(0, NT // 2) as j:
            load_shared(j * 2, 0)
            load_shared(j * 2 + 1, 1)

        sp.wait_ge(scattered, 16 * 2 * NT)
        sp.wait_ge(rt_done, 1)
        pairs = sp.value_load(ends[0:1, E:E + 1], min_val=NT, max_val=BLOCKS // 2)

        def slots(i, par, on):
            if on[0]:
                sp.wait_ge(f["xT"], C + i - 1)
                sp.dma_start(xf_sb[par][:, :], slot_tiles[bass.ds(i - NT, 1)].rearrange("t p d -> p (t d)")).then_inc(f_x[par], 16)
            if on[2]:
                sp.wait_ge(f["y"], C + i - 1)
                sp.dma_start(slot_out[bass.ds(i - 2 - NT, 1)].rearrange("t p d -> p (t d)"), y_sb[par][:, :]).then_inc(f_st[par], 16)

        sweep(sp, NT, pairs, slots)

        sp.wait_ge(g_done, 16 * NT)

    @block.gpsimd
    def _(pool):
        for s in credited:
            pool.sem_inc(s, C)
        pool.dma_start(bias1[0:1, :], sb1.rearrange("(o n) -> o n", o=1)).then_inc(ld["bias"], 16)
        pool.dma_start(bias1[1:E + 1, :], eb1).then_inc(ld["bias"], 16)
        pool.dma_start(bias2[0:1, :], sb2.rearrange("(o n) -> o n", o=1)).then_inc(ld["bias"], 16)
        pool.dma_start(bias2[1:E + 1, :], eb2).then_inc(ld["bias"], 16)
        pool.dma_start(bias2[E + 1:E + 2, :], xb.rearrange("(o n) -> o n", o=1)).then_inc(ld["bias"], 16)
        pool.dma_start(rw_sb[:, :, :], rw.rearrange("(c p) e -> p c e", p=P)).then_inc(ld["small"], 16)
        pool.dma_start(rb_sb[:, :], rb.rearrange("(o n) -> o n", o=1)).then_inc(ld["small"], 16)
        pool.dma_start(b_out[:, :], xb.rearrange("(o n) -> o n", o=1).broadcast_to([P, D])).then_inc(ld["small"], 16)
        steps = 0

        def did(ins):
            nonlocal steps
            steps += 1
            ins.then_inc(made_steps, 1)

        did(pool.memset(ident[:, :], 0.0))
        did(pool.memset(identb[:, :], 0.0))
        did(pool.memset(ones[:, :], 1.0))
        did(pool.memset(onesb[:, :], 1.0))
        did(pool.memset(before[:, :], 1.0))
        did(pool.memset(minus_half[:, :], -0.5))
        did(pool.memset(window[:, :], 0.0))
        did(pool.memset(vinit[:, :, :], 1.0))
        did(pool.memset(lastk[:, :, :], 0.0))
        pool.wait_ge(made_steps, steps)
        for m in (ident, identb):
            did(pool.affine_select(out=m[:, :], in_=m[:, :], compare_op=ALU.not_equal, fill=1.0,
                                   base=0, pattern=[[-1, P]], channel_multiplier=1))
        did(pool.affine_select(out=before[:, :], in_=before[:, :], compare_op=ALU.is_gt, fill=0.0,
                               base=0, pattern=[[1, P]], channel_multiplier=-1))
        owns = window[:, 0:P], window[:, P + 2 * W:]
        prev = window[:, P:P + 2 * W].rearrange("p (n w) -> p n w", n=2)
        for own in owns:
            did(pool.affine_select(out=own, in_=own, compare_op=ALU.is_ge, fill=MASKED, base=0,
                                   pattern=[[-1, P]], channel_multiplier=1))
        did(pool.affine_select(out=prev, in_=prev, compare_op=ALU.is_ge, fill=MASKED, base=-1,
                               pattern=[[0, 2], [1, W]], channel_multiplier=-1))
        pool.wait_ge(made_steps, steps)
        for own in owns:
            did(pool.affine_select(out=own, in_=own, compare_op=ALU.is_ge, fill=MASKED, base=W - 1,
                                   pattern=[[1, P]], channel_multiplier=-1))
        did(pool.memset(qs[:, :, :], 0.0))
        did(pool.memset(ks[:, :, :], 0.0))
        did(pool.memset(KB[:, :, :, :], 0.0))
        did(pool.memset(VB[:, :, :, :], 0.0))
        pool.wait_ge(made_steps, steps)
        pool.dma_start(vinit[1:W, :, 0:DH], last_v).then_inc(ld["lastv"], 16)
        pool.dma_start(vinit[W + 1:P, :, 0:DH], last_v).then_inc(ld["lastv"], 16)
        pool.wait_ge(ld["lastv"], 32)
        pool.wait_ge(ld["last"], 16)
        pool.sem_inc(made, 1)
        pool.wait_ge(ks_hi, 1)
        pool.tensor_copy(ks[0:W, :, 32:48], ks[0:W, :, 0:16]).then_inc(ks_dup, 1)
        pool.wait_ge(p_pe, CHUNKS)
        pool.wait_ge(p_act, CHUNKS)
        pool.wait_ge(ks_dup, 1)
        for i in range(2):
            pool.memset(V[i][:, :, :], 1.0).then_inc(made, 1)
        for i in range(2):
            pool.wait_ge(made, 3 + 2 * i)
            pool.memset(qe[i][64:P, :, :].bitcast(F32), 0.0).then_inc(made, 1)
            pool.wait_ge(made, 4 + 2 * i)
            pool.memset(qo[i][0:64, :, :].bitcast(F32), 0.0).then_inc(made, 1)
        pool.wait_ge(made, 7)
        for i in range(2):
            pool.memset(vprev[i][:, :, :], 0.0).then_inc(made, 1)

        def inverse_deviation(st, s, t):
            pool.wait_ge(s, C + t * 4 + 3)
            pool.tensor_tensor(st[:, 8:9], st[:, 7:8], minus_half[:, :], ALU.pow).then_inc(s, 1)

        def dup(t):
            inverse_deviation(stats, a["ln"], t)
            pool.wait_ge(a["hi"], C + t + 1)
            pass_waits(pool)
            pool.tensor_copy(qs[:, :, 16:32], qs[:, :, 0:16]).then_inc(a["dup"], 1)
            pool.tensor_copy(ks[:, :, 32:48], ks[:, :, 0:16]).then_inc(a["dup"], 1)

        with pool.Fori(0, NT) as t:
            dup(t)

        def split_weights(g):
            if g <= 2:
                pool.wait_ge(ld_raw, 32 * (g + 1))
            else:
                pool.wait_ge(ld_raw_pool, 32 * (g - 2))
            high, low = wts[:, g % 2, 0, :], wts[:, g % 2, 1, :]
            pool.tensor_copy(high, raw[:, :]).then_inc(w_split, 1)
            pool.wait_ge(w_split, 2 * g + 1)
            pool.tensor_tensor(low, raw[:, :], high.bitcast(F32), ALU.subtract).then_inc(w_split, 1)

        pool.wait_ge(a["x1"], C + NT)
        split_weights(0)

        def cross(i, par, on):
            if on[0]:
                inverse_deviation(stats2, c["ln"], i)
            if on[1]:
                t = i - 1
                pool.wait_ge(c["xn"], C + t + 1)
                xt = X[:, bass.ds(t, 1), :].rearrange("p t d -> p (t d)")
                pool.tensor_tensor(xt, xt, b_out[:, :], ALU.add).then_inc(c["bo"], 1)
            if on[2]:
                inverse_deviation(stats2, c["ln3"], i - 2)
            if on[1]:
                pool.wait_ge(c["rd"], C + t + 1)
                pr = prob2[1 - par][:, :, :]
                pool.tensor_tensor(pr, pr, den2[:, 1, :].unsqueeze(2).broadcast_to([P, XH, CK]), ALU.mult).then_inc(c["nrm"], 1)

        sweep(pool, 0, NT // 2, cross, 4)
        pool.wait_ge(c["x2"], C + NT)
        pool.wait_ge(c["lgc"], C + NT)
        pool.memset(zeros[:, :], 0.0).then_inc(z_made, 1)
        pool.iota(iota8[:, :], pattern=[[1, E]], base=0, channel_multiplier=0,
                  allow_small_or_imprecise_dtypes=True).then_inc(rt_idx, 1)
        pool.wait_ge(rt_idx, 1)
        pool.iota(iotab[:, :], pattern=[[1, BLOCKS]], base=0, channel_multiplier=0,
                  allow_small_or_imprecise_dtypes=True).then_inc(rt_idx, 1)
        pool.wait_ge(rt_idx, 2)
        split_weights(1)
        pool.wait_ge(zeroed, 16 * (2 * BLOCKS - 2 * NT))
        pool.wait_ge(rt_done, 1)
        for t in range(NT):
            for k in range(2):
                pool.indirect_dma_start(slot_x, bass.IndirectOffsetOnAxis(dest[:, k, t:t + 1], 0),
                                        XN3[:, t, :], None).then_inc(scattered, 16)
        for g in range(2, E + 1):
            if g == 2:
                pool.wait_ge(f["dn"], C + NT)
            else:
                e = pool.value_load(ends[0:1, g - 3:g - 2], min_val=0, max_val=BLOCKS)
                pool.wait_ge(f["dn"], e + (C + NT))
                pass_waits(pool)
            split_weights(g)
            if g < E:
                pool.wait_ge(w_split, 2 * (g + 1))
                pool.dma_start(raw[:, 0:DC * FF].rearrange("p (c f) -> p c f", c=DC),
                               ew1[g].rearrange("(c p) f -> p c f", p=P)).then_inc(ld_raw_pool, 16)
                pool.dma_start(raw[:, DC * FF:].rearrange("p (c n) -> p c n", c=KF),
                               ew2[g].rearrange("(c p) n -> p c n", p=P)).then_inc(ld_raw_pool, 16)

        pairs = pool.value_load(ends[0:1, E:E + 1], min_val=NT, max_val=BLOCKS // 2)
        pool.wait_ge(f_st[0], pairs * 16 + C)
        pool.wait_ge(f_st[1], pairs * 16 + C)
        pass_waits(pool)
        for t in range(NT):
            if t >= 2:
                pool.wait_ge(g_add, 2 * (t - 1))
            pool.indirect_dma_start(ya[t % 2][:, :], None, slot_y,
                                    bass.IndirectOffsetOnAxis(dest[:, 0, t:t + 1], 0)).then_inc(g_y[t % 2], 16)
            pool.indirect_dma_start(yb[t % 2][:, :], None, slot_y,
                                    bass.IndirectOffsetOnAxis(dest[:, 1, t:t + 1], 0)).then_inc(g_y[t % 2], 16)


    self_qkv, self_s, self_t = PQ[0], PQ[1], PQ[2]
    self_o = PQ[3][:, 0, 0:H * VROW]
    self_m = PQ[3][:, 1, :]
    BANKS = ((PQ[0][:, 0, :], 0, 6), (PQ[0][:, 1, :], 6, 12), (PQ[1][:, 0, :], 12, XH))
    cross_x = PQ[1][:, 1, :]
    cross_t = (PQ[2][:, 0, :], PQ[2][:, 1, :], PQ[3][:, 0, :])
    TCH = ((0, 4), (4, 8), (8, FC))
    cross_o = PQ[3][:, 1, 0:D]
    cross_l = PQ[3][:, 1, D:D + E]
    up_banks = (PQ[0], PQ[3])
    down_t = PQ[1]
    down_y = PQ[2][:, 0, 0:D]
    ffn_x = PQ[2][:, 1, 0:D]

    def tile_of(t):
        return X[:, bass.ds(t, 1), :].rearrange("p t d -> p (t d)")

    def heads_of(u):
        g, r = u // 2, u % 2
        return r, (2 * g, 2 * g + 1)

    @block.tensor
    def _(pe):
        def begins(n):
            if n >= 4:
                pe.wait_ge(p_act, n - 3)
                pe.wait_ge(p_dve, n - 3)
            return PQ[n % 4]

        pe.wait_ge(made, 1)
        pe.wait_ge(ld["w4"], 64)
        for ch in range(DC):
            ps = begins(CH_WT + ch)
            for n in range(4):
                for r in range(DC):
                    last = pe.transpose(ps[:, n // 2, n % 2 * D + r * P:n % 2 * D + (r + 1) * P],
                                        w4[:, n, r, ch * P:(ch + 1) * P], ident[:, :])
            last.then_inc(p_pe, 1)
        pe.wait_ge(ld["ctx"], 16)
        ps = begins(CH_CT)
        for b in range(B):
            pe.transpose(ps[:, 0, b * CK:(b + 1) * CK], ctx_sb[:, b, 0:P], ident[0:CK, 0:CK])
            last = pe.transpose(ps[0:CD - P, 1, b * CK:(b + 1) * CK], ctx_sb[:, b, P:CD], ident[0:CK, 0:CK])
        last.then_inc(p_pe, 1)
        pe.wait_ge(ks_dup, 1)
        pe.wait_ge(ks_lo, 1)
        ps = begins(CH_KI)
        for p in range(H // 2):
            last = pe.transpose(ps[:, p // 4, p % 4 * W:(p % 4 + 1) * W],
                                ks[0:W, 2 * p:2 * p + 2, :].rearrange("p h k -> p (h k)"), ident[0:W, 0:W])
        last.then_inc(p_pe, 1)
        pe.wait_ge(ld["xq"], 16)
        for ch in range(2):
            ps = begins(CH_WQ + ch)
            for p in range(4):
                for r in range(DC):
                    last = pe.transpose(ps[:, p // 2, p % 2 * D + r * P:p % 2 * D + (r + 1) * P],
                                        xq_sb[:, r, (4 * ch + p) * P:(4 * ch + p + 1) * P], ident[:, :])
            last.then_inc(p_pe, 1)
        pe.wait_ge(p_act, CH_CT + 1)
        pe.wait_ge(p_dve, CH_CT + 1)
        for first, w_sb, s in ((CH_K, xk_sb, "xk"), (CH_V, xv_sb, "xv")):
            pe.wait_ge(ld[s], 32)
            for ch in range(2):
                ps = begins(first + ch)
                for p in range(4):
                    o = ps[:, p // 2, p % 2 * B * CK:(p % 2 + 1) * B * CK]
                    at = (4 * ch + p) * P
                    pe.matmul(o, w_sb[:, 0, at:at + P], cT[:, 0, :], start=True, stop=False)
                    last = pe.matmul(o, w_sb[0:CD - P, 1, at:at + P], cT[0:CD - P, 1, :], start=False, stop=True)
                last.then_inc(p_pe, 1)
        pe.wait_ge(p_act, CH_K + 2)
        pe.wait_ge(p_dve, CH_K + 2)
        for n in range(8):
            b, ch, half = n // 4, n // 2 % 2, n % 2
            ps = begins(CH_A + n)
            for p in range(4):
                last = pe.matmul(ps[:, p // 2, p % 2 * 2 * CK:(p % 2 + 1) * 2 * CK],
                                 wqT[:, 4 * half + p, ch * P:(ch + 1) * P], KB[:, b, 4 * half + p, :],
                                 start=True, stop=True)
            last.then_inc(p_pe, 1)
        pe.wait_ge(ld["xo"], 16)
        pe.wait_ge(p_act, CH_V + 2)
        pe.wait_ge(p_dve, CH_V + 2)
        for n, (b, c0) in enumerate(VW_CH):
            ps = begins(CH_VW + n)
            for ch in range(c0, min(c0 + 4, FC)):
                M = vw_rows(ch)
                o = ps[0:M, (ch - c0) // 2, (ch - c0) % 2 * D:((ch - c0) % 2 + 1) * D]
                over = [p for p in range(HP) if 2 * CK * p < ch * P + M and 2 * CK * (p + 1) > ch * P]
                for p in over:
                    at = P + ch * P - 2 * CK * p
                    last = pe.matmul(o, VB[:, p, b, at:at + M], xo_sb[:, p, :],
                                     start=p == over[0], stop=p == over[-1])
            last.then_inc(p_pe, 1)

        pe.wait_ge(p_act, CHUNKS)
        pe.wait_ge(p_dve, CHUNKS)
        pe.wait_ge(made, 9)

        def self_attention(i, par, on):
            for u in range(10):
                if on[1] and u < 8:
                    if u == 0:
                        for s in ("qE", "qO", "kA", "kD"):
                            pe.wait_ge(a[s], C + i)
                    pe.wait_ge(a["exp"], C + (i - 1) * 8 + u - 1)
                    r, pairs = heads_of(u)
                    ps = self_s[:, u % 2, 0:2 * KW]
                    pe.matmul(ps, identb[:, :], window[:, :], start=True, stop=False)
                    for n, p in enumerate(pairs):
                        q = (qe, qo)[r][1 - par][:, p, :]
                        own, prev = (0, KW + W)[n], (P, KW)[n]
                        pe.matmul(ps[:, own:own + P], q, kst[1 - par][:, p, :], start=False, stop=False)
                        last = pe.matmul(ps[:, prev:prev + W], q, kst[par][:, p, P - W:P],
                                         start=False, stop=n == 1)
                    last.then_inc(a["S"], 1)
                if on[2] and u == 1:
                    pe.wait_ge(a["on"], C + i - 1)
                    pe.wait_ge(a["x1"], C + i - 2)
                    for ch in range(DC):
                        last = pe.transpose(self_m[:, ch * P:(ch + 1) * P], o_sb[:, ch * P:(ch + 1) * P], ident[:, :])
                    last.then_inc(a["oT"], 1)
                if on[0] and u == 1:
                    pe.wait_ge(a["xn"], C + i + 1)
                    pe.wait_ge(a["kA"], C + i)
                    pe.wait_ge(a["kD"], C + i)
                    for ch in range(DC):
                        last = pe.transpose(self_qkv[:, 0, ch * P:(ch + 1) * P], xn[:, ch * P:(ch + 1) * P], ident[:, :])
                    last.then_inc(a["xT"], 1)
                if on[2] and u == 3:
                    pe.wait_ge(a["oh"], C + i - 1)
                    pe.wait_ge(a["ol"], C + i - 1)
                    for ch in range(DC):
                        last = split_product(pe, self_m[:, D:2 * D], (oth[:, ch, :], otl[:, ch, :]),
                                             (WTh[:, ch, 3 * D:4 * D], WTl[:, ch, 3 * D:4 * D]), ch == 0, ch == 1)
                    last.then_inc(a["op"], 1)
                if on[0] and u == 3:
                    pe.wait_ge(a["xh"], C + i + 1)
                    pe.wait_ge(a["xl"], C + i + 1)
                    for o, lo, hi in ((self_qkv[:, 0, :], 0, 2 * D), (self_qkv[:, 1, 0:D], 2 * D, 3 * D)):
                        for ch in range(DC):
                            last = split_product(pe, o, (xth[:, ch, :], xtl[:, ch, :]),
                                                 (WTh[:, ch, lo:hi], WTl[:, ch, lo:hi]), ch == 0, ch == 1)
                    last.then_inc(a["qkv"], 1)
                if on[0] and u == 5:
                    pe.wait_ge(a["lo"], C + i + 1)
                    pe.wait_ge(a["v"], C + i + 1)
                    pe.wait_ge(a["dup"], C + (i + 1) * 2)
                    for p in range(H // 2):
                        last = pe.transpose(self_qkv[:, p // 4, p % 4 * P:(p % 4 + 1) * P],
                                            qs[:, 2 * p:2 * p + 2, :].rearrange("p h k -> p (h k)"), ident[:, :])
                    last.then_inc(a["qT"], 1)
                if on[0] and u == 8:
                    pe.wait_ge(a["qE"], C + i + 1)
                    pe.wait_ge(a["qO"], C + i + 1)
                    for p in range(H // 2):
                        last = pe.transpose(self_qkv[:, p // 4, p % 4 * P:(p % 4 + 1) * P],
                                            ks[:, 2 * p:2 * p + 2, :].rearrange("p h k -> p (h k)"), ident[:, :])
                    last.then_inc(a["kT"], 1)
                w = u - 1
                if on[1] and 0 <= w < 8:
                    pe.wait_ge(a["exp"], C + (i - 1) * 8 + w + 1)
                    pe.wait_ge(a[f"ev{w % 2}"], C + (i - 1) * 4 + w // 2)
                    for n in range(3):
                        last = pe.transpose(self_t[:, w % 2, n * P:(n + 1) * P], prob[w % 2][:, n * P:(n + 1) * P], ident[:, :])
                    last.then_inc(a["tr"], 1)
                w = u - 2
                if on[1] and 0 <= w < 8:
                    pe.wait_ge(a[f"ev{w % 2}"], C + (i - 1) * 4 + w // 2 + 1)
                    if w == 0:
                        pe.wait_ge(a["on"], C + i - 1)
                        pe.wait_ge(a["v"], C + i)
                        pe.wait_ge(a_vp[1 - par], (i + par) * 16 + C)
                    r, pairs = heads_of(w)
                    for n, p in enumerate(pairs):
                        h = 2 * p + r
                        o = self_o[:, h * VROW:(h + 1) * VROW]
                        pe.matmul(o, pt[w % 2][:, 2 * n, :], V[1 - par][:, h, :], start=True, stop=False)
                        last = pe.matmul(o, pt[w % 2][:, 1, :], vprev[1 - par][:, h, :], start=False, stop=True)
                    last.then_inc(a["pv"], 1)

        with pe.Fori(0, B) as b:
            pe.wait_ge(a_k0, b + 1)
            sweep(pe, b * TB, TB // 2, self_attention)

        pe.wait_ge(a["x1"], C + NT)

        def cross(i, par, on):
            if on[1]:
                batch = bass.ds((i - 1) // TB, 1)
                pe.wait_ge(c["xh"], C + i)
                pe.wait_ge(c["xl"], C + i)
                for k, (ps, h0, h1) in enumerate(BANKS):
                    pe.wait_ge(c["exp"], C + (i - 2) * 3 + k + 1)
                    for ch in range(DC):
                        right = [m[:, batch, ch, h0 * CK:h1 * CK].rearrange("p b n -> p (b n)") for m in (Ah, Al)]
                        last = split_product(pe, ps[:, 0:(h1 - h0) * CK], (xt2h[:, ch, :], xt2l[:, ch, :]),
                                             right, ch == 0, ch == 1)
                    last.then_inc(c["S"], 1)
            if on[2]:
                pe.wait_ge(c["nrm"], C + i - 1)
                flat = prob2[par][:, :, :].rearrange("p h k -> p (h k)")
                for k, (c0, c1) in enumerate(TCH):
                    pe.wait_ge(c["pl"], C + (i - 3) * 3 + k + 1)
                    for n in range(c0, c1):
                        M = vw_rows(n)
                        last = pe.transpose(cross_t[k][0:M, (n - c0) * P:(n - c0 + 1) * P], flat[:, n * P:n * P + M], ident[:, :])
                    last.then_inc(c["pT"], 1)
            if on[0]:
                pe.wait_ge(c["xn"], C + i + 1)
                pe.wait_ge(c["x3"], C + i - 3)
                pe.wait_ge(c["xl"], C + i)
                for ch in range(DC):
                    last = pe.transpose(cross_x[:, ch * P:(ch + 1) * P], xn2[:, ch * P:(ch + 1) * P], ident[:, :])
                last.then_inc(c["xT"], 1)
            if on[3]:
                pe.wait_ge(c["xn3"], C + i - 2)
                if on[0]:
                    pe.wait_ge(c["xl"], C + i + 1)
                for ch in range(DC):
                    last = pe.transpose(cross_x[:, D + ch * P:D + (ch + 1) * P],
                                        XN3c[:, ch * P:(ch + 1) * P], ident[:, :])
                last.then_inc(c["x3T"], 1)
            if on[2]:
                batch = bass.ds((i - 2) // TB, 1)
                pe.wait_ge(c["x2"], C + i - 2)
                pe.wait_ge(c["lgc"], C + i - 4)
                for k, (c0, c1) in enumerate(TCH):
                    pe.wait_ge(c["pl"], C + (i - 2) * 3 + k + 1)
                    for n in range(c0, c1):
                        M = vw_rows(n)
                        right = [m[0:M, batch, n, :].rearrange("p b d -> p (b d)") for m in (VWh, VWl)]
                        last = split_product(pe, cross_o, (pth[0:M, n, :], ptl[0:M, n, :]), right, n == 0, n == FC - 1)
                last.then_inc(c["o"], 1)
            if on[3]:
                pe.wait_ge(c["x3"], C + i - 2)
                pe.wait_ge(c["lgc"], C + i - 3)
                if on[2]:
                    pe.wait_ge(c["x2"], C + i - 1)
                pe.matmul(cross_l, ones[0:1, :], rb_sb[:, :], start=True, stop=False)
                for ch in range(DC):
                    last = pe.matmul(cross_l, x3t[:, ch, :], rw_sb[:, ch, :], start=False, stop=ch == 1)
                last.then_inc(c["lg"], 1)

        pe.wait_ge(ld["small"], 48)
        sweep(pe, 0, NT // 2, cross, 4)

        pe.wait_ge(rt, RT_SEL)
        pe.matmul(rank_ps, before[:, :], sel.rearrange("p t e -> p (t e)"), start=True, stop=True).then_inc(rt_pe, 1)
        pe.matmul(total_ps, ones[:, :], sel.rearrange("p t e -> p (t e)"), start=True, stop=True).then_inc(rt_pe, 1)

        def experts(routed):
            def body(i, par, on):
                def weights_of(block, rows):
                    if not routed:
                        return (lambda part, lo, n: wts[:, 0, part, lo:lo + n]), (lambda n, at: rows[0:3, at:at + n])
                    width = FF if rows is b1r else D
                    at_block = bass.ds(block - NT, 1)
                    stage = pe.value_load(stage_of[0:1, at_block], min_val=1, max_val=E)
                    place = pe.value_load(place_of[0:1, at_block], min_val=0, max_val=1)
                    if rows is b1r:
                        pe.wait_ge(w_split, stage * 2 + 2)
                    return (lambda part, lo, n: wts[:, bass.ds(place, 1), part, lo:lo + n].rearrange("p o n -> p (o n)"),
                            lambda n, at: rows[0:3, bass.ds(stage * width + at, n)])

                if on[1]:
                    weight, bias = weights_of(i - 1, b1r)
                    pe.wait_ge(f["xh"], C + i)
                    pe.wait_ge(f["xl"], C + i)
                    pe.wait_ge(f["act"], C + i - 2)
                    ps = up_banks[1 - par]
                    for n in range(2):
                        pe.matmul(ps[:, n, :], onesb[0:3, :], bias(512, n * 512), start=True, stop=False)
                    for ch in range(DC):
                        for part in range(2):
                            for n in range(2):
                                pe.matmul(ps[:, n, :], fxh[:, ch, :], weight(part, ch * FF + n * 512, 512), start=False, stop=False)
                        for n in range(2):
                            last = pe.matmul(ps[:, n, :], fxl[:, ch, :], weight(0, ch * FF + n * 512, 512), start=False, stop=ch == 1)
                    last.then_inc(f["up"], 1)
                if on[0]:
                    pe.wait_ge(f_x[par], (i - par) * 8 + 16)
                    pe.wait_ge(f["xl"], C + i)
                    for ch in range(DC):
                        last = pe.transpose(ffn_x[:, ch * P:(ch + 1) * P], xf_sb[par][:, ch * P:(ch + 1) * P], ident[:, :])
                    last.then_inc(f["xT"], 1)
                if on[2]:
                    weight, bias = weights_of(i - 2, b2r)
                    pe.wait_ge(f["hl"], C + (i - 1) * 2)
                    pe.wait_ge(f["y"], C + i - 2)
                    pe.matmul(down_y, onesb[0:3, :], bias(D, 0), start=True, stop=False)
                    for k in range(KF):
                        last = split_product(pe, down_y, (hth[:, k, :], htl[:, k, :]),
                                             [weight(part, DC * FF + k * D, D) for part in range(2)], False, k == KF - 1)
                    last.then_inc(f["dn"], 1)
                if on[1]:
                    pe.wait_ge(f["act"], C + i)
                    pe.wait_ge(f["hl"], C + (i - 1) * 2)
                    for n in range(2):
                        for k in range(4):
                            last = pe.transpose(down_t[:, n, k * P:(k + 1) * P], hact[:, (4 * n + k) * P:(4 * n + k + 1) * P], ident[:, :])
                        last.then_inc(f["hT"], 1)
            return body

        pe.wait_ge(ld["b1r"], 32)
        pe.wait_ge(w_split, 2)
        sweep(pe, 0, NT // 2, experts(False))
        pe.wait_ge(rt_done, 1)
        pairs = pe.value_load(ends[0:1, E:E + 1], min_val=NT, max_val=BLOCKS // 2)
        sweep(pe, NT, pairs, experts(True))

    @block.scalar
    def _(act):
        def copy(o, i, scale=1.0):
            return nc.scalar.activation(o, i, ACT.Copy, scale=scale)

        act.wait_ge(made, 1)
        copy(ks[0:W, :, 0:16].bitcast(F32R), lastk[:, :, :]).then_inc(ks_hi, 1)
        for ch in range(DC):
            act.wait_ge(p_pe, CH_WT + ch + 1)
            copy(WTh[:, ch, :].rearrange("p (a n) -> p a n", a=2), PQ[CH_WT + ch][:, :, :]).then_inc(p_act, 1)
        act.wait_ge(p_pe, CH_CT + 1)
        copy(cT[:, 0, :], PQ[CH_CT % 4][:, 0, 0:B * CK]).then_inc(p_act, 1)
        act.wait_ge(p_pe, CH_KI + 1)
        copy(kinit[:, 0:4, :], PQ[CH_KI % 4][:, 0, 0:4 * W].rearrange("p (a w) -> p a w", a=4)).then_inc(p_act, 1)
        for ch in range(2):
            act.wait_ge(p_pe, CH_WQ + ch + 1)
            copy(wqT[:, 4 * ch:4 * ch + 2, :], PQ[(CH_WQ + ch) % 4][:, 0, :].rearrange("p (a d) -> p a d", a=2)).then_inc(p_act, 1)
        for first in (CH_K, CH_V):
            for ch in range(2):
                act.wait_ge(p_pe, first + ch + 1)
                for q in range(2):
                    for r in range(2):
                        half = slice(r * XD, (r + 1) * XD)
                        src = PQ[(first + ch) % 4][half, 0, q * B * CK:(q + 1) * B * CK].rearrange("p (b k) -> p b k", b=B)
                        p = 4 * ch + q
                        if first == CH_K:
                            last = copy(KB[half, :, p, r * CK:(r + 1) * CK], src, XD ** -0.5)
                        else:
                            last = copy(VB[half, p, :, P + r * CK:P + (r + 1) * CK], src)
                last.then_inc(p_act, 1)
        for n in range(8):
            b, ch, half = n // 4, n // 2 % 2, n % 2
            act.wait_ge(p_pe, CH_A + n + 1)
            copy(Ah[:, b, ch, half * HALF:(half + 1) * HALF].rearrange("p (a n) -> p a n", a=2),
                 PQ[(CH_A + n) % 4][:, :, 0:HALF // 2]).then_inc(p_act, 1)
        for n, (b, c0) in enumerate(VW_CH):
            act.wait_ge(p_pe, CH_VW + n + 1)
            ps = PQ[(CH_VW + n) % 4]
            if c0 + 4 <= FC:
                last = copy(VWh[:, b, c0:c0 + 4, :].rearrange("p (a c) d -> p a (c d)", a=2), ps[:, :, :])
            else:
                copy(VWh[:, b, c0, :], ps[:, 0, 0:D])
                last = copy(VWh[0:FLAST, b, c0 + 1, :], ps[0:FLAST, 0, D:2 * D])
            last.then_inc(p_act, 1)

        act.wait_ge(p_pe, CHUNKS)
        act.wait_ge(made, 9)

        def self_attention(i, par, on):
            for u in range(10):
                if on[1] and u < 8:
                    act.wait_ge(a["max"], C + (i - 1) * 8 + u + 1)
                    act.wait_ge(a["tr"], C + (i - 1) * 8 + u - 1)
                    r, pairs = heads_of(u)
                    for n, p in enumerate(pairs):
                        h = 2 * p + r
                        last = nc.scalar.activation(prob[u % 2][:, n * KW:(n + 1) * KW], self_s[:, u % 2, n * KW:(n + 1) * KW],
                                                    ACT.Exp, bias=negm[:, 1 - par, h:h + 1])
                    last.then_inc(a["exp"], 1)
                if on[2] and u == 1:
                    act.wait_ge(a["oT"], C + i - 1)
                    copy(oth[:, :, :], self_m[:, 0:D].rearrange("p (c n) -> p c n", c=DC)).then_inc(a["oh"], 1)
                if on[0] and u == 2:
                    act.wait_ge(a["xT"], C + i + 1)
                    copy(xth[:, :, :], self_qkv[:, 0, 0:D].rearrange("p (c n) -> p c n", c=DC)).then_inc(a["xh"], 1)
                if on[0] and u == 4:
                    act.wait_ge(a["qkv"], C + i + 1)
                    act.wait_ge(a["pv"], C + i * 8 - 8)
                    act.wait_ge(a_vp[1 - par], (i + par) * 16 + C)
                    copy(qs[:, :, 0:16].bitcast(F32R), self_qkv[:, 0, 0:D].rearrange("p (h d) -> p h d", h=H), DH ** -0.5)
                    copy(ks[:, :, 0:16].bitcast(F32R), self_qkv[:, 0, D:2 * D].rearrange("p (h d) -> p h d", h=H)).then_inc(a["hi"], 1)
                    copy(V[par][:, :, 0:DH], self_qkv[:, 1, 0:D].rearrange("p (h d) -> p h d", h=H)).then_inc(a["v"], 1)
                if on[0] and u == 6:
                    act.wait_ge(a["qT"], C + i + 1)
                    copy(qe[par][0:64, :, :].rearrange("p (a c) n -> p a (c n)", a=2), self_qkv[0:64, :, :]).then_inc(a["qE"], 1)
                w = u - 1
                if on[1] and 0 <= w < 8 and w % 2:
                    act.wait_ge(a["tr"], C + (i - 1) * 8 + w + 1)
                    act.wait_ge(a["pv"], C + (i - 1) * 8 + w - 1)
                    copy(pt[1][:, :, :], self_t[:, 1, 0:3 * P].rearrange("p (a n) -> p a n", a=3)).then_inc(a["ev1"], 1)
                if on[0] and u == 9:
                    act.wait_ge(a["kT"], C + i + 1)
                    copy(kst[par][:, 0:4, :], self_qkv[:, 0, :].rearrange("p (c n) -> p c n", c=4)).then_inc(a["kA"], 1)

        with act.Fori(0, B) as b:
            sweep(act, b * TB, TB // 2, self_attention)

        act.wait_ge(a["x1"], C + NT)

        def cross(i, par, on):
            if on[2]:
                for k, (c0, c1) in enumerate(TCH):
                    act.wait_ge(c["pT"], C + (i - 2) * 3 + k + 1)
                    if k < 2:
                        last = copy(pth[:, c0:c1, :], cross_t[k].rearrange("p (a n) -> p a n", a=4))
                    else:
                        copy(pth[:, c0, :], cross_t[k][:, 0:P])
                        last = copy(pth[0:FLAST, c0 + 1, :], cross_t[k][0:FLAST, P:2 * P])
                    last.then_inc(c["ph"], 1)
            if on[0]:
                act.wait_ge(c["xT"], C + i + 1)
                copy(xt2h[:, :, :], cross_x[:, 0:D].rearrange("p (c n) -> p c n", c=DC)).then_inc(c["xh"], 1)
            if on[1]:
                act.wait_ge(c["nrm"], C + i - 3 + 1)
                act.wait_ge(c["pT"], C + (i - 2) * 3)
                for k, (ps, h0, h1) in enumerate(BANKS):
                    act.wait_ge(c["max"], C + (i - 1) * 3 + k + 1)
                    for h in range(h0, h1):
                        last = nc.scalar.activation(prob2[1 - par][:, h, :], ps[:, (h - h0) * CK:(h - h0 + 1) * CK], ACT.Exp,
                                                    bias=negm2[:, h:h + 1], accum_out=den2[:, 0, h:h + 1])
                    last.then_inc(c["exp"], 1)
            if on[3]:
                act.wait_ge(c["x3T"], C + i - 2)
                copy(x3t[:, :, :], cross_x[:, D:2 * D].rearrange("p (c n) -> p c n", c=DC)).then_inc(c["x3"], 1)

        sweep(act, 0, NT // 2, cross, 4)

        act.wait_ge(rt, RT_SHIFTED)
        nc.scalar.activation(e8[1][:, :, :], e8[0][:, :, :], ACT.Exp).then_inc(rt_act, 1)

        def experts(routed):
            def body(i, par, on):
                if on[1]:
                    act.wait_ge(f["up"], C + i)
                    act.wait_ge(f["hT"], C + (i - 1) * 2)
                    nc.scalar.activation(hact[:, :].rearrange("p (a n) -> p a n", a=2), up_banks[1 - par][:, :, :], ACT.Gelu).then_inc(f["act"], 1)
                if on[0]:
                    act.wait_ge(f["xT"], C + i + 1)
                    copy(fxh[:, :, :], ffn_x.rearrange("p (c n) -> p c n", c=DC)).then_inc(f["xh"], 1)
                if on[2] and routed:
                    act.wait_ge(f["dn"], C + i - 1)
                    act.wait_ge(f_st[par], (i - par - 2 - NT) * 8 + C)
                    copy(y_sb[par][:, :], down_y).then_inc(f["y"], 1)
                if on[1]:
                    for n in range(2):
                        act.wait_ge(f["hT"], C + (i - 1) * 2 + n + 1)
                        copy(hth[:, 4 * n:4 * n + 4, :], down_t[:, n, :].rearrange("p (a n) -> p a n", a=4)).then_inc(f["hh"], 1)
            return body

        sweep(act, 0, NT // 2, experts(False))
        act.wait_ge(rt_done, 1)
        pairs = act.value_load(ends[0:1, E:E + 1], min_val=NT, max_val=BLOCKS // 2)
        sweep(act, NT, pairs, experts(True))
        for t in range(NT):
            act.wait_ge(g_add, 2 * (t + 1))
            act.dma_start(of[:, t, :], X[:, t, :]).then_inc(g_done, 16)

    @block.vector
    def _(dve):
        def less_high(o, whole, high):
            return dve.tensor_tensor(o, whole, high.bitcast(F32), ALU.subtract)

        steps = 0

        def step(ins):
            nonlocal steps
            steps += 1
            ins.then_inc(p_steps, 1)
            dve.wait_ge(p_steps, steps)

        dve.wait_ge(ks_hi, 1)
        less_high(ks[0:W, :, 16:32], lastk[:, :, :], ks[0:W, :, 0:16]).then_inc(ks_lo, 1)
        dve.wait_ge(ld["bias"], 80)
        for whole, parts in ((bias1, bias1p), (bias2, bias2p)):
            step(dve.tensor_copy(parts[:, 0, :], whole[:, :]))
            dve.sem_inc(bias_split, 1)
            step(dve.tensor_tensor(whole[:, :], whole[:, :], parts[:, 0, :], ALU.subtract))
            step(dve.tensor_copy(parts[:, 1, :], whole[:, :]))
            dve.sem_inc(bias_split, 1)
            step(dve.tensor_tensor(whole[:, :], whole[:, :], parts[:, 1, :], ALU.subtract))
            step(dve.tensor_copy(parts[:, 2, :], whole[:, :]))
            dve.sem_inc(bias_split, 1)
        for ch in range(DC):
            dve.wait_ge(p_act, CH_WT + ch + 1)
            less_high(WTl[:, ch, :].rearrange("p (a n) -> p a n", a=2), PQ[CH_WT + ch][:, :, :],
                      WTh[:, ch, :].rearrange("p (a n) -> p a n", a=2)).then_inc(p_dve, 1)
        dve.wait_ge(p_pe, CH_CT + 1)
        dve.tensor_copy(cT[0:CD - P, 1, :], PQ[CH_CT % 4][0:CD - P, 1, 0:B * CK]).then_inc(p_dve, 1)
        dve.wait_ge(p_pe, CH_KI + 1)
        dve.tensor_copy(kinit[:, 4:8, :], PQ[CH_KI % 4][:, 1, 0:4 * W].rearrange("p (a w) -> p a w", a=4)).then_inc(p_dve, 1)
        for ch in range(2):
            dve.wait_ge(p_pe, CH_WQ + ch + 1)
            dve.tensor_copy(wqT[:, 4 * ch + 2:4 * ch + 4, :], PQ[(CH_WQ + ch) % 4][:, 1, :].rearrange("p (a d) -> p a d", a=2)).then_inc(p_dve, 1)
        for first in (CH_K, CH_V):
            for ch in range(2):
                dve.wait_ge(p_pe, first + ch + 1)
                for q in range(2):
                    for r in range(2):
                        half = slice(r * XD, (r + 1) * XD)
                        src = PQ[(first + ch) % 4][half, 1, q * B * CK:(q + 1) * B * CK].rearrange("p (b k) -> p b k", b=B)
                        p = 4 * ch + 2 + q
                        if first == CH_K:
                            last = dve.tensor_scalar(KB[half, :, p, r * CK:(r + 1) * CK], src, XD ** -0.5, None, ALU.mult)
                        else:
                            last = dve.tensor_copy(VB[half, p, :, P + r * CK:P + (r + 1) * CK], src)
                last.then_inc(p_dve, 1)
        for n in range(8):
            b, ch, half = n // 4, n // 2 % 2, n % 2
            cols = slice(half * HALF, (half + 1) * HALF)
            dve.wait_ge(p_act, CH_A + n + 1)
            less_high(Al[:, b, ch, cols].rearrange("p (a n) -> p a n", a=2), PQ[(CH_A + n) % 4][:, :, 0:HALF // 2],
                      Ah[:, b, ch, cols].rearrange("p (a n) -> p a n", a=2)).then_inc(p_dve, 1)
        dve.wait_ge(ld["brow"], 96)
        for n, (b, c0) in enumerate(VW_CH):
            dve.wait_ge(p_act, CH_VW + n + 1)
            ps = PQ[(CH_VW + n) % 4]
            if c0 + 4 <= FC:
                last = less_high(VWl[:, b, c0:c0 + 4, :].rearrange("p (a c) d -> p a (c d)", a=2), ps[:, :, :],
                                 VWh[:, b, c0:c0 + 4, :].rearrange("p (a c) d -> p a (c d)", a=2))
            else:
                less_high(VWl[:, b, c0, :], ps[:, 0, 0:D], VWh[:, b, c0, :])
                last = less_high(VWl[0:FLAST, b, c0 + 1, :], ps[0:FLAST, 0, D:2 * D], VWh[0:FLAST, b, c0 + 1, :])
            last.then_inc(p_dve, 1)

        def layer_norm(o, xt, st, s, t, free, freed):
            pass_waits(dve)
            dve.bn_stats(st[:, 0:6], xt).then_inc(s, 1)
            dve.wait_ge(s, C + t * 4 + 1)
            pass_waits(dve)
            dve.bn_aggr(st[:, 6:8], st[:, 0:6]).then_inc(s, 1)
            dve.wait_ge(s, C + t * 4 + 2)
            dve.tensor_scalar(st[:, 7:8], st[:, 7:8], EPS, None, ALU.add).then_inc(s, 1)
            dve.wait_ge(s, C + t * 4 + 4)
            if free is not None:
                dve.wait_ge(free, freed)
            return dve.tensor_scalar(o, xt, st[:, 6:7], st[:, 8:9], ALU.subtract, ALU.mult)

        dve.wait_ge(p_pe, CHUNKS)
        dve.wait_ge(made, 9)
        dve.wait_ge(ld["x"], 16)

        def self_attention(i, par, on):
            for u in range(10):
                if on[1] and u < 8:
                    dve.wait_ge(a["S"], C + (i - 1) * 8 + u + 1)
                    h = 4 * (u // 2) + u % 2
                    dve.tensor_reduce(negm[:, 1 - par, h:h + 3:2], self_s[:, u % 2, 0:2 * KW].rearrange("p (n k) -> p n k", n=2),
                                      AX.X, ALU.max, negate=True).then_inc(a["max"], 1)
                if on[2] and u == 0:
                    dve.wait_ge(a["pv"], C + (i - 1) * 8)
                    dve.wait_ge(a["oT"], C + i - 2)
                    o3 = self_o.rearrange("p (h v) -> p h v", h=H)
                    dve.reciprocal(rden[:, :].unsqueeze(2), o3[:, :, DH:VROW]).then_inc(a["rd"], 1)
                    dve.wait_ge(a["rd"], C + i - 1)
                    dve.tensor_tensor(o_sb[:, :].rearrange("p (h d) -> p h d", h=H), o3[:, :, 0:DH],
                                      rden[:, :].unsqueeze(2).broadcast_to([P, H, DH]), ALU.mult).then_inc(a["on"], 1)
                if on[0] and u == 0:
                    layer_norm(xn[:, :], tile_of(i), stats, a["ln"], i, a["xT"], C + i).then_inc(a["xn"], 1)
                if on[2] and u == 2:
                    dve.wait_ge(a["oh"], C + i - 1)
                    less_high(otl[:, :, :], self_m[:, 0:D].rearrange("p (c n) -> p c n", c=DC), oth[:, :, :]).then_inc(a["ol"], 1)
                if on[0] and u == 2:
                    dve.wait_ge(a["xh"], C + i + 1)
                    less_high(xtl[:, :, :], self_qkv[:, 0, 0:D].rearrange("p (c n) -> p c n", c=DC), xth[:, :, :]).then_inc(a["xl"], 1)
                if on[2] and u == 4:
                    dve.wait_ge(a["op"], C + i - 1)
                    xt = tile_of(i - 2)
                    dve.tensor_tensor(xt, self_m[:, D:2 * D], xt, ALU.add).then_inc(a["x1"], 1)
                if on[0] and u == 4:
                    dve.wait_ge(a["hi"], C + i + 1)
                    dve.scalar_tensor_tensor(qs[:, :, 32:48], self_qkv[:, 0, 0:D].rearrange("p (h d) -> p h d", h=H), DH ** -0.5,
                                             qs[:, :, 0:16], ALU.mult, ALU.subtract)
                    less_high(ks[:, :, 16:32], self_qkv[:, 0, D:2 * D].rearrange("p (h d) -> p h d", h=H), ks[:, :, 0:16]).then_inc(a["lo"], 1)
                if on[0] and u == 6:
                    dve.wait_ge(a["qT"], C + i + 1)
                    dve.tensor_copy(qo[par][64:P, :, :].rearrange("p (a c) n -> p a (c n)", a=2), self_qkv[64:P, :, :]).then_inc(a["qO"], 1)
                w = u - 1
                if on[1] and 0 <= w < 8 and w % 2 == 0:
                    dve.wait_ge(a["tr"], C + (i - 1) * 8 + w + 1)
                    dve.wait_ge(a["pv"], C + (i - 1) * 8 + w - 1)
                    dve.tensor_copy(pt[0][:, :, :], self_t[:, 0, 0:3 * P].rearrange("p (a n) -> p a n", a=3)).then_inc(a["ev0"], 1)
                if on[0] and u == 9:
                    dve.wait_ge(a["kT"], C + i + 1)
                    dve.tensor_copy(kst[par][:, 4:8, :], self_qkv[:, 1, :].rearrange("p (c n) -> p c n", c=4)).then_inc(a["kD"], 1)

        with dve.Fori(0, B) as b:
            dve.wait_ge(a["S"], b * (8 * TB) + C)
            dve.tensor_copy(kst[1][:, :, P - W:P], kinit[:, :, :]).then_inc(a_k0, 1)
            sweep(dve, b * TB, TB // 2, self_attention)

        dve.wait_ge(a["x1"], C + NT)
        dve.wait_ge(ld["small"], 48)

        def cross(i, par, on):
            if on[0]:
                layer_norm(xn2[:, :], tile_of(i), stats2, c["ln"], i, c["xT"], C + i).then_inc(c["xn"], 1)
            if on[1]:
                dve.wait_ge(c["exp"], C + (i - 1) * 3)
                for k, (ps, h0, h1) in enumerate(BANKS):
                    dve.wait_ge(c["S"], C + (i - 1) * 3 + k + 1)
                    dve.tensor_reduce(negm2[:, h0:h1], ps[:, 0:(h1 - h0) * CK].rearrange("p (h k) -> p h k", k=CK),
                                      AX.X, ALU.max, negate=True).then_inc(c["max"], 1)
            if on[2]:
                for k, (c0, c1) in enumerate(TCH):
                    dve.wait_ge(c["ph"], C + (i - 2) * 3 + k + 1)
                    if k < 2:
                        last = less_high(ptl[:, c0:c1, :], cross_t[k].rearrange("p (a n) -> p a n", a=4), pth[:, c0:c1, :])
                    else:
                        less_high(ptl[:, c0, :], cross_t[k][:, 0:P], pth[:, c0, :])
                        last = less_high(ptl[0:FLAST, c0 + 1, :], cross_t[k][0:FLAST, P:2 * P], pth[0:FLAST, c0 + 1, :])
                    last.then_inc(c["pl"], 1)
            if on[0]:
                dve.wait_ge(c["xh"], C + i + 1)
                less_high(xt2l[:, :, :], cross_x[:, 0:D].rearrange("p (c n) -> p c n", c=DC), xt2h[:, :, :]).then_inc(c["xl"], 1)
            if on[2]:
                t = i - 2
                dve.wait_ge(c["o"], C + t + 1)
                dve.wait_ge(c["bo"], C + t + 1)
                xt = tile_of(t)
                dve.tensor_tensor(xt, cross_o, xt, ALU.add).then_inc(c["x2"], 1)
                dve.wait_ge(c["x2"], C + t + 1)
                layer_norm(XN3c[:, :], xt, stats2, c["ln3"], t, c["x3T"], C + t).then_inc(c["xn3"], 1)
                dve.wait_ge(c["xn3"], C + t + 1)
                dve.tensor_copy(XN3[:, bass.ds(t, 1), :].rearrange("p t d -> p (t d)"), XN3c[:, :]).then_inc(c["x3c"], 1)
            if on[3]:
                dve.wait_ge(c["lg"], C + i - 2)
                dve.tensor_copy(logits[:, bass.ds(i - 3, 1), :].rearrange("p t e -> p (t e)"), cross_l).then_inc(c["lgc"], 1)
            if on[1]:
                dve.wait_ge(c["exp"], C + i * 3)
                dve.wait_ge(c["nrm"], C + i - 1)
                dve.reciprocal(den2[:, 1, :], den2[:, 0, :]).then_inc(c["rd"], 1)

        sweep(dve, 0, NT // 2, cross, 4)

        done = 0

        def route(ins):
            nonlocal done
            done += 1
            ins.then_inc(rt, 1)
            dve.wait_ge(rt, done)

        def over_experts(m):
            return m.unsqueeze(2).broadcast_to([P, NT, E])

        shifted, expd, hot0, hot1, sel_, dest8 = (m[:, :, :] for m in e8)
        peak, total, rtotal = (m[:, :] for m in s16[0:3])
        dve.wait_ge(c["lgc"], C + NT)
        route(dve.tensor_reduce(peak, logits[:, :, :], AX.X, ALU.max))
        route(dve.tensor_tensor(shifted, logits[:, :, :], over_experts(peak), ALU.subtract))
        assert done == RT_SHIFTED
        dve.wait_ge(rt_act, 1)
        route(dve.tensor_reduce(total, expd, AX.X, ALU.add))
        route(dve.reciprocal(rtotal, total))
        route(dve.tensor_tensor(shifted, expd, over_experts(rtotal), ALU.mult))
        for t in range(NT):
            last = dve.max(best[:, t, :], shifted[:, t, :])
        route(last)
        for t in range(NT):
            last = dve.max_index(besti[:, t, :], best[:, t, :], shifted[:, t, :])
        route(last)
        route(dve.tensor_copy(bestf[:, :, :], besti[:, :, 0:2]))
        dve.wait_ge(rt_idx, 2)
        every = iota8[:, :].unsqueeze(1).broadcast_to([P, NT, E])
        dve.tensor_tensor(hot0, every, bestf[:, :, 0:1].broadcast_to([P, NT, E]), ALU.is_equal)
        route(dve.tensor_tensor(hot1, every, bestf[:, :, 1:2].broadcast_to([P, NT, E]), ALU.is_equal))
        route(dve.tensor_tensor(sel_, hot0, hot1, ALU.add))
        assert done == RT_SEL
        route(dve.tensor_tensor(total, best[:, :, 0], best[:, :, 1], ALU.add))
        route(dve.tensor_scalar(total, total, 1e-9, None, ALU.add))
        route(dve.reciprocal(rtotal, total))
        route(dve.tensor_tensor(gate[:, :, :], best[:, :, 0:2], rtotal.unsqueeze(2).broadcast_to([P, NT, 2]), ALU.mult))
        dve.wait_ge(rt_pe, 2)
        tot3 = total_ps.rearrange("p (t e) -> p t e", e=E)
        route(dve.tensor_copy(run[0][:, :, :], tot3))
        route(dve.tensor_copy(run0, tot3))
        src, span = 0, 1
        while span < NT:
            dve.tensor_copy(run[1 - src][:, 0:span, :], run[src][:, 0:span, :])
            route(dve.tensor_tensor(run[1 - src][:, span:NT, :], run[src][:, span:NT, :], run[src][:, 0:NT - span, :], ALU.add))
            src, span = 1 - src, span * 2
        count = run[src][:, NT - 1, :]
        route(dve.tensor_scalar(counts[0][:, :], count, float(P - 1), None, ALU.add))
        route(dve.tensor_copy(countsi[0][:, :], counts[0][:, :]))
        route(dve.tensor_scalar(countsi[1][:, :], countsi[0][:, :], P.bit_length() - 1, None, ALU.arith_shift_right))
        route(dve.tensor_copy(counts[3][:, :], countsi[1][:, :]))
        route(dve.tensor_copy(counts[0][:, :], counts[3][:, :]))
        at, span = 0, 1
        while span < E:
            dve.tensor_copy(counts[1 - at][:, 0:span], counts[at][:, 0:span])
            route(dve.tensor_tensor(counts[1 - at][:, span:E], counts[at][:, span:E], counts[at][:, 0:E - span], ALU.add))
            at, span = 1 - at, span * 2
        end, first = counts[at][:, :], counts[2][:, :]
        route(dve.tensor_tensor(first, end, counts[3][:, :], ALU.subtract))
        route(dve.tensor_scalar(first, first, float(P), None, ALU.mult))
        route(dve.tensor_tensor(dest8, run[src][:, :, :], run0, ALU.subtract))
        route(dve.tensor_tensor(dest8, rank_ps.rearrange("p (t e) -> p t e", e=E), dest8, ALU.add))
        route(dve.tensor_tensor(dest8, dest8, first.unsqueeze(1).broadcast_to([P, NT, E]), ALU.add))
        for k, hot in enumerate((hot0, hot1)):
            route(dve.tensor_tensor(hot, hot, dest8, ALU.mult))
            route(dve.tensor_reduce(destf[:, k, :], hot, AX.X, ALU.add))
        route(dve.tensor_copy(dest[:, :, :], destf[:, :, :]))
        route(dve.tensor_tensor(owner8[:, :, :], iotab[:, :].unsqueeze(2).broadcast_to([1, BLOCKS, E]),
                                end[0:1, :].unsqueeze(1).broadcast_to([1, BLOCKS, E]), ALU.is_ge))
        route(dve.tensor_reduce(owner[0][:, :], owner8[:, :, :], AX.X, ALU.add))
        route(dve.tensor_scalar(owner[0][:, :], owner[0][:, :], float(E - 1), 1.0, ALU.min, ALU.add))
        route(dve.tensor_copy(stage_of[:, :], owner[0][:, :]))
        route(dve.tensor_scalar(place_of[:, :], stage_of[:, :], 1, None, ALU.bitwise_and))
        route(dve.tensor_copy(ends[0:1, 0:E], end[0:1, :]))
        route(dve.tensor_scalar(owner[1][0:1, 0:1], end[0:1, E - 1:E], 1.0, None, ALU.add))
        route(dve.tensor_copy(ends[0:1, E:E + 1], owner[1][0:1, 0:1]))
        route(dve.tensor_scalar(pairs_i[:, :], ends[0:1, E:E + 1], 1, None, ALU.arith_shift_right))
        dve.tensor_copy(ends[0:1, E:E + 1], pairs_i[:, :]).then_inc(rt_done, 1)

        def experts(routed):
            def body(i, par, on):
                if on[0]:
                    dve.wait_ge(f["xh"], C + i + 1)
                    less_high(fxl[:, :, :], ffn_x.rearrange("p (c n) -> p c n", c=DC), fxh[:, :, :]).then_inc(f["xl"], 1)
                if on[2] and not routed:
                    dve.wait_ge(f["dn"], C + i - 1)
                    xt = tile_of(i - 2)
                    dve.tensor_tensor(xt, down_y, xt, ALU.add).then_inc(f["y"], 1)
                if on[1]:
                    for n in range(2):
                        dve.wait_ge(f["hh"], C + (i - 1) * 2 + n + 1)
                        less_high(htl[:, 4 * n:4 * n + 4, :], down_t[:, n, :].rearrange("p (a n) -> p a n", a=4),
                                  hth[:, 4 * n:4 * n + 4, :]).then_inc(f["hl"], 1)
            return body

        sweep(dve, 0, NT // 2, experts(False))
        dve.wait_ge(rt_done, 1)
        pairs = dve.value_load(ends[0:1, E:E + 1], min_val=NT, max_val=BLOCKS // 2)
        sweep(dve, NT, pairs, experts(True))
        for t in range(NT):
            dve.wait_ge(g_y[t % 2], 32 * (t // 2 + 1))
            dve.scalar_tensor_tensor(X[:, t, :], ya[t % 2][:, :], gate[:, t, 0:1], X[:, t, :], ALU.mult, ALU.add).then_inc(g_add, 1)
            dve.wait_ge(g_add, 2 * t + 1)
            dve.scalar_tensor_tensor(X[:, t, :], yb[t % 2][:, :], gate[:, t, 1:2], X[:, t, :], ALU.mult, ALU.add).then_inc(g_add, 1)

    block_ctx.__exit__(None, None, None)


_INS = ['x', 'ctx_768', 'L0_attn_Wq', 'L0_attn_Wk', 'L0_attn_Wv', 'L0_attn_Wo', 'L0_attn_last_k_init',
        'L0_attn_last_v_init', 'L0_xattn_w_q', 'L0_xattn_w_k', 'L0_xattn_w_v', 'L0_xattn_w_out',
        'L0_xattn_b_out', 'L0_ffn_shared_w1', 'L0_ffn_shared_b1', 'L0_ffn_shared_w2', 'L0_ffn_shared_b2',
        'L0_ffn_router_w', 'L0_ffn_router_b', 'L0_ffn_exp_w1', 'L0_ffn_exp_b1', 'L0_ffn_exp_w2',
        'L0_ffn_exp_b2']
_OUTS = [((2, 1024, 256), 'float32')]


def kernel(**inputs):
    import numpy as _np
    import concourse.bacc as _bacc
    from concourse import mybir as _mybir
    from concourse.bass_utils import run_bass_kernel_spmd as _run

    nc = _bacc.Bacc("TRN2", target_bir_lowering=False, num_devices=1)
    arrays, args = {}, []
    for name in _INS:
        a = _np.ascontiguousarray(inputs[name])
        arrays[f"in_{name}_dram"] = a
        args.append(nc.dram_tensor(f"in_{name}_dram", a.shape, _mybir.dt.from_np(a.dtype), kind="ExternalInput").ap())
    for i, (shape, dtype) in enumerate(_OUTS):
        dt = _mybir.dt.from_np(_np.dtype(dtype))
        args.append(nc.dram_tensor(f"out_{i}_dram", shape, dt, kind="ExternalOutput").ap())
    decoder_layer(nc, *args)
    r = _run(nc, [arrays], core_ids=[0])
    return r.results[0]["out_0_dram"]
```

```python
import numpy as np
import concourse.bass as bass
from concourse import mybir
from concourse.alu_op_type import AluOpType as ALU

ACT = mybir.ActivationFunctionType
AX = mybir.AxisListType
F32 = mybir.dt.float32
F32R = mybir.dt.float32r
BF16 = mybir.dt.bfloat16
I32 = mybir.dt.int32
U32 = mybir.dt.uint32

P = 128
EPS = 1e-5
MASKED = -1e30
CREDIT = 64


class Region:

    def __init__(self, nc, start, end):
        self.nc, self.at, self.end = nc, start, end

    def place(self, name, shape, dtype):
        size = int(np.prod(shape[1:])) * (2 if dtype == BF16 else 4)
        t = self.nc.alloc_sbuf_tensor_at(name, shape, dtype, offset=self.at)
        self.at += (size + 63) // 64 * 64
        assert self.at <= self.end, (name, self.at, self.end)
        return t


def sweep(eng, base, pairs, body, stages=3, beside=()):
    lag = stages // 2 * 2
    for k in range(lag):
        body(base + k, k % 2, [n <= k for n in range(stages)])
        if k < len(beside):
            beside[k]()
    with eng.Fori(lag // 2, pairs) as j:
        body(base + j * 2, 0, [True] * stages)
        body(base + j * 2 + 1, 1, [True] * stages)
    for k in range(stages - 1):
        body(base + pairs * 2 + k, k % 2, [n > k for n in range(stages)])


def decoder_layer(nc, x, ctx, wq, wk, wv, wo, last_k, last_v, xq, xk, xv, xo, xb,
                  sw1, sb1, sw2, sb2, rw, rb, ew1, eb1, ew2, eb2, out):
    B, L, D = x.shape
    TOK = B * L
    NT = TOK // P
    TB = L // P
    W1, H, DH = last_k.shape
    W = W1 + 1
    DC = D // P
    CK, CD = ctx.shape[1:]
    XA = xq.shape[1]
    XH = 16
    XD = XA // XH
    HP = XA // P
    FL = XH * CK
    FC = -(-FL // P)
    FLAST = FL - (FC - 1) * P
    E, _, FF = ew1.shape
    KF = FF // P
    BLOCKS = (2 * TOK) // P + E
    HROW = 32
    HG = H * HROW // P
    KW = P + W

    b1_rows = nc.dram_tensor("b1_rows", [3, E + 1, FF], BF16, kind="Internal").ap()
    b2_rows = nc.dram_tensor("b2_rows", [3, E + 2, D], BF16, kind="Internal").ap()
    slot_x = nc.dram_tensor("slot_x", [BLOCKS * P, D], F32, kind="Internal").ap()
    slot_y = nc.dram_tensor("slot_y", [BLOCKS * P, D], F32, kind="Internal").ap()

    xf = x.rearrange("b l d -> (b l) d").rearrange("(t p) d -> p t d", p=P)
    of = out.rearrange("b l d -> (b l) d").rearrange("(t p) d -> p t d", p=P)

    base = (nc.sbuf_base + 63) // 64 * 64
    top = nc.sbuf_usable_end
    keep = Region(nc, base, base + 24 * 1024)
    X = keep.place("X", [P, NT, D], F32)
    ident = keep.place("ident", [P, P], F32)
    identb = keep.place("identb", [P, P], BF16)
    window = keep.place("window", [P, 2 * KW], BF16)
    ones = keep.place("ones", [P, P], F32)
    onesb = keep.place("onesb", [P, P], BF16)
    before = keep.place("before", [P, P], F32)
    rw_sb = keep.place("rw_sb", [P, DC, E], F32)
    rb_sb = keep.place("rb_sb", [1, E], F32)
    minus_half = keep.place("minus_half", [P, 1], F32)
    b_out = keep.place("b_out", [P, D], F32)
    zeros = keep.place("zeros", [P, D], F32)

    r1 = keep.at
    R1 = 48 * 1024
    r2 = r1 + R1
    R2 = 157 * 512
    r3 = r2 + R2

    PLACES = 3
    WN = 2 * KF * D
    reg = Region(nc, r1, r3)
    raw = reg.place("raw", [P, WN], F32)
    wts = reg.place("wts", [P, PLACES, 2, WN], F32R)
    hth = reg.place("hth", [P, KF, P], F32R)
    htl = reg.place("htl", [P, KF, P], F32R)

    reg = Region(nc, r2, r3)
    Ah = reg.place("Ah", [P, B, DC, FL], F32R)
    Al = reg.place("Al", [P, B, DC, FL], F32R)
    VWh = reg.place("VWh", [P, B, FC, D], F32R)
    VWl = reg.place("VWl", [P, B, FC, D], F32R)

    reg = Region(nc, r3, top)
    WTh = reg.place("WTh", [P, DC, 3 * D], F32R)
    WTl = reg.place("WTl", [P, DC, 3 * D], F32R)
    WOh = reg.place("WOh", [P, HG, D], F32R)
    WOl = reg.place("WOl", [P, HG, D], F32R)
    kinit = reg.place("kinit", [P, H // 2, W], F32R)
    vinit = reg.place("vinit", [P, H, HROW], F32)
    qs = reg.place("qs", [P, H, 64], F32)
    ks = reg.place("ks", [P, H, 64], F32)
    r3b = reg.at
    xn = reg.place("xn", [P, D], F32)
    xth = reg.place("xth", [P, DC, P], F32R)
    xtl = reg.place("xtl", [P, DC, P], F32R)
    stats = reg.place("stats", [P, 16], F32)
    idle = Region(nc, r1 + 4 * WN, r2)
    qe = [idle.place(f"qe{i}", [P, H // 2, P], F32R) for i in range(2)]
    qo = [idle.place(f"qo{i}", [P, H // 2, P], F32R) for i in range(2)]
    kst = [idle.place(f"kst{i}", [P, H // 2, W + KW], F32R) for i in range(2)]
    V = [reg.place(f"V{i}", [P, H, HROW], F32) for i in range(2)]
    vprev = [reg.place(f"vprev{i}", [P, H, HROW], F32) for i in range(2)]
    negm = reg.place("negm", [P, 2, H], F32)
    prob = [reg.place(f"prob{i}", [P, 2 * KW], F32) for i in range(4)]
    pt = [reg.place(f"pt{i}", [P, 3, P], F32) for i in range(2)]
    den = reg.place("den", [P, 2, H], F32)
    rden = reg.place("rden", [P, H, HROW], F32)
    o_sb = reg.place("o_sb", [P, HG, P], F32)
    oth = reg.place("oth", [P, HG, P], F32R)
    otl = reg.place("otl", [P, HG, P], F32R)

    reg = Region(nc, r1, r2)
    wqT = reg.place("wqT", [P, HP, D], F32)
    xo_sb = reg.place("xo_sb", [P, HP, D], F32)
    KB = reg.place("KB", [P, B, HP, 2 * CK], F32)
    xk_sb = reg.place("xk_sb", [P, 2, XA], F32)
    cT = reg.place("cT", [P, 2, B * CK], F32)
    ctx_sb = reg.place("ctx_sb", [CK, B, CD], F32)
    lastk = reg.place("lastk", [W, H, DH], F32)
    reg = Region(nc, r3b, top)
    VZ = P + 2 * CK + P
    VB = reg.place("VB", [P, HP, B, VZ], F32)
    reg = Region(nc, r2, r3)
    xv_sb = reg.place("xv_sb", [P, 2, XA], F32)
    w4 = reg.place("w4", [P, 4, DC, D], F32)
    xq_sb = reg.place("xq_sb", [P, DC, XA], F32)
    wo_pad = reg.place("wo_pad", [P, DC, H, HROW], F32)
    reg = Region(nc, r2 + 2 * 4 * B * DC * FL + 4 * B * FC * D, r3)
    bias1 = reg.place("bias1", [E + 1, FF], F32)
    bias1p = reg.place("bias1p", [E + 1, 3, FF], BF16)
    bias2 = reg.place("bias2", [E + 2, D], F32)
    bias2p = reg.place("bias2p", [E + 2, 3, D], BF16)

    top2 = (top - 2 * (E + 1) * FF) // 64 * 64
    reg = Region(nc, r3, top2)
    XN3 = reg.place("XN3", [P, NT, D], F32)
    r3c = reg.at
    logits = reg.place("logits", [P, NT, E], F32)
    XN3c = reg.place("XN3c", [P, D], F32)
    xn2 = reg.place("xn2", [P, D], F32)
    xt2h = reg.place("xt2h", [P, DC, P], F32R)
    xt2l = reg.place("xt2l", [P, DC, P], F32R)
    negm2 = reg.place("negm2", [P, XH], F32)
    den2 = reg.place("den2", [P, 2, XH], F32)
    prob2 = [reg.place(f"prob2_{i}", [P, XH, CK], F32) for i in range(2)]
    pth = reg.place("pth", [P, FC, P], F32R)
    ptl = reg.place("ptl", [P, FC, P], F32R)
    x3t = reg.place("x3t", [P, DC, P], F32)
    stats2 = reg.place("stats2", [P, 16], F32)
    stats3 = reg.place("stats3", [P, 16], F32)

    b1r = Region(nc, top2, top).place("b1r", [3, (E + 1) * FF], BF16)
    reg = Region(nc, r3c + NT * E * 4, top2)
    b2r = reg.place("b2r", [3, (E + 2) * D], BF16)
    xf_sb = [reg.place(f"xf{i}", [P, D], F32) for i in range(2)]
    fxh = reg.place("fxh", [P, DC, P], F32R)
    fxl = reg.place("fxl", [P, DC, P], F32R)
    hact = reg.place("hact", [P, FF], F32)
    y_sb = [reg.place(f"y{i}", [P, D], F32) for i in range(2)]
    e8 = [reg.place(f"e8_{i}", [P, NT, E], F32) for i in range(6)]
    s16 = [reg.place(f"s16_{i}", [P, NT], F32) for i in range(4)]
    run = [reg.place(f"run{i}", [P, NT, E], F32) for i in range(3)]
    pairs_i = reg.place("pairs_i", [1, 1], I32)
    best = reg.place("best", [P, NT, 8], F32)
    besti = reg.place("besti", [P, NT, 8], U32)
    bestf = reg.place("bestf", [P, NT, 2], F32)
    gate = reg.place("gate", [P, NT, 2], F32)
    destf = reg.place("destf", [P, 2, NT], F32)
    dest = reg.place("dest", [P, 2, NT], I32)
    iota8 = reg.place("iota8", [P, E], F32)
    iotab = reg.place("iotab", [1, BLOCKS], F32)
    counts = [reg.place(f"counts{i}", [P, E], F32) for i in range(4)]
    countsi = [reg.place(f"countsi{i}", [P, E], I32) for i in range(2)]
    owner8 = reg.place("owner8", [1, BLOCKS, E], F32)
    owner = [reg.place(f"owner{i}", [1, BLOCKS], F32) for i in range(2)]
    stage_of = reg.place("stage_of", [1, BLOCKS], I32)
    place_of = reg.place("place_of", [1, BLOCKS], I32)
    ends = reg.place("ends", [1, E + 1], I32)
    ya = Region(nc, r3, r3c).place("ya", [P, NT, D], F32)
    yb = Region(nc, r1, r1 + 4 * WN).place("yb", [P, NT, D], F32)

    PQ = [nc.alloc_psum_tensor(f"PQ{i}", [P, 2, 512], F32) for i in range(4)]

    RT_SHIFTED, RT_SEL = 2, 10
    sel = e8[4][:, :, :]
    rank_ps, total_ps = PQ[0][:, 0, 0:NT * E], PQ[0][:, 1, 0:NT * E]
    run0 = run[2][:, :, :]

    sems = {}

    def sem(name):
        sems[name] = nc.alloc_semaphore(name)
        return sems[name]

    def split_product(pe, o, left, right, start, stop):
        (lh, ll), (rh, rl) = left, right
        pe.matmul(o, lh, rh, start=start, stop=False)
        pe.matmul(o, lh, rl, start=False, stop=False)
        return pe.matmul(o, ll, rh, start=False, stop=stop)

    passed = sem("passed")

    def pass_waits(eng):
        eng.sem_inc(passed, 1)

    ld = {n: sem("ld_" + n) for n in ("x", "w4", "ctx", "last", "lastv", "xq", "xk", "xv", "xo", "bias",
                                      "small", "brow", "b1r")}
    made = sem("made")
    made_steps = sem("made_steps")
    v_made = sem("v_made")
    kv_made = sem("kv_made")
    p_pe, p_act, p_dve = sem("p_pe"), sem("p_act"), sem("p_dve")
    p_steps = sem("p_steps")
    bias_split = sem("bias_split")
    wo_padded = sem("wo_padded")
    ks_hi, ks_lo, ks_dup = sem("ks_hi"), sem("ks_lo"), sem("ks_dup")
    a_names = ("ln", "xn", "xT", "xh", "xl", "qkv", "hi", "lo", "v", "qT", "qE", "qO", "kT",
               "kA", "kD", "pA", "pD", "S", "max", "exp", "tr", "ev0", "ev1", "pv", "rc", "rd", "rT", "rS", "on", "oh",
               "ol", "op", "x1")
    a = {n: sem("a_" + n) for n in a_names}
    a_vp = [sem("a_vp0"), sem("a_vp1")]
    a_k0 = sem("a_k0")
    c_names = ("ln", "xn", "xT", "xh", "xl", "S", "max", "sub", "exp", "sum", "rd", "nrm", "pT", "ph", "pl", "o",
               "x2", "bo", "ln3", "xn3", "x3c", "x3T", "x3", "lg", "lgc", "wh", "wl")
    c = {n: sem("c_" + n) for n in c_names}
    rt, rt_act, rt_pe, rt_idx, rt_done = (sem(n) for n in ("rt", "rt_act", "rt_pe", "rt_idx", "rt_done"))
    ld_raw, ld_raw_pool, w_split = sem("ld_raw"), sem("ld_raw_pool"), sem("w_split")
    zeroed, scattered, z_made = sem("zeroed"), sem("scattered"), sem("z_made")
    f_names = ("xT", "xh", "xl", "up", "act", "hT", "hh", "hl", "dn", "y")
    f = {n: sem("f_" + n) for n in f_names}
    f_x = [sem("f_x0"), sem("f_x1")]
    f_st = [sem("f_st0"), sem("f_st1")]
    g_y = [sem(f"g_y{t}") for t in range(NT)]
    g_add, g_done, g_mid = sem("g_add"), sem("g_done"), sem("g_mid")
    credited = [*a.values(), *c.values(), *f.values(), *a_vp, *f_st]
    C = CREDIT

    block_ctx = nc.Block()
    block = block_ctx.__enter__()

    CH_WT, CH_WO, CH_CT, CH_KI, CH_WQ, CH_K, CH_V, CH_A, CH_VW = 0, 2, 3, 4, 5, 7, 9, 11, 19
    CHUNKS = 25
    HALF = FL // 2
    VW_CH = [(b, n) for b in range(B) for n in range(0, FC, 4)]

    def vw_rows(n):
        return P if n < FC - 1 else FLAST

    @block.sync
    def _(sp):
        for n, w in enumerate((wq, wk, wv, wo)):
            sp.dma_start(w4[:, n, :, :], w.rearrange("(c p) i -> p c i", p=P)).then_inc(ld["w4"], 16)
        sp.wait_ge(made_steps, 12)
        sp.dma_start(lastk[1:W, :, :], last_k).then_inc(ld["last"], 16)
        sp.dma_start(ctx_sb[:, :, :], ctx.rearrange("b k d -> k b d")).then_inc(ld["ctx"], 16)
        sp.dma_start(vinit[1:W, :, 0:DH], last_v).then_inc(ld["lastv"], 16)
        sp.dma_start(vinit[W + 1:P, :, 0:DH], last_v).then_inc(ld["lastv"], 16)
        sp.dma_start(xq_sb[:, :, :], xq.rearrange("(c p) n -> p c n", p=P)).then_inc(ld["xq"], 16)
        for t, w, s in ((xk_sb, xk, "xk"), (xv_sb, xv, "xv")):
            sp.dma_start(t[:, 0, :], w[0:P, :]).then_inc(ld[s], 16)
            sp.dma_start(t[0:CD - P, 1, :], w[P:CD, :]).then_inc(ld[s], 16)
        sp.dma_start(xo_sb[:, :, :], xo.rearrange("(c p) n -> p c n", p=P)).then_inc(ld["xo"], 16)
        sp.dma_start(X[:, :, :], xf).then_inc(ld["x"], 16)
        sp.wait_ge(bias_split, 6)
        for r in range(3):
            sp.dma_start(b1_rows[r], bias1p[:, r, :]).then_inc(ld["brow"], 16)
            sp.dma_start(b2_rows[r], bias2p[:, r, :]).then_inc(ld["brow"], 16)
        sp.wait_ge(p_pe, CHUNKS)
        sp.dma_start(raw[:, 0:DC * FF].rearrange("p (c f) -> p c f", c=DC),
                     sw1.rearrange("(c p) f -> p c f", p=P)).then_inc(ld_raw, 16)
        sp.dma_start(raw[:, DC * FF:].rearrange("p (c n) -> p c n", c=KF),
                     sw2.rearrange("(c p) n -> p c n", p=P)).then_inc(ld_raw, 16)

        def prev_values(t, k):
            sp.wait_ge(a["pv"], C + 8 * t - 8)
            pass_waits(sp)
            if k == 0:
                sp.wait_ge(made, 3)
                sp.wait_ge(v_made, 6)
                src = vinit[W:P, :, :]
            else:
                sp.wait_ge(a["v"], C + t)
                src = V[1 - k % 2][W:P, :, :]
            for n in range(2):
                half = vprev[k % 2][n * W:(n + 1) * W, n:H:2, :]
                sp.dma_start(half, src[:, n:H:2, :]).then_inc(a_vp[k % 2], 16)

        with sp.Fori(0, B) as b:
            prev_values(b * TB, 0)
            prev_values(b * TB + 1, 1)
            with sp.Fori(1, TB // 2) as j:
                prev_values(b * TB + j * 2, 2)
                prev_values(b * TB + j * 2 + 1, 3)

        sp.wait_ge(a["x1"], C + NT)
        sp.wait_ge(ld["brow"], 16 * 6)
        sp.dma_start(b1r[:, :], b1_rows.rearrange("r e f -> r (e f)")).then_inc(ld["b1r"], 16)
        sp.wait_ge(z_made, 1)
        slot_tiles = slot_x.rearrange("(t p) d -> t p d", p=P)
        with sp.Fori(0, BLOCKS) as t:
            sp.dma_start(slot_tiles[bass.ds(t, 1)].rearrange("t p d -> p (t d)"), zeros[:, :]).then_inc(zeroed, 16)
        slot_out = slot_y.rearrange("(t p) d -> t p d", p=P)
        with sp.Fori(2 * NT, BLOCKS) as t:
            sp.dma_start(slot_out[bass.ds(t, 1)].rearrange("t p d -> p (t d)"), zeros[:, :]).then_inc(zeroed, 16)

        def raw_weights(e):
            sp.wait_ge(w_split, 2 * (e + 1))
            sp.dma_start(raw[:, 0:DC * FF].rearrange("p (c f) -> p c f", c=DC),
                         ew1[e].rearrange("(c p) f -> p c f", p=P)).then_inc(ld_raw, 16)
            sp.dma_start(raw[:, DC * FF:].rearrange("p (c n) -> p c n", c=KF),
                         ew2[e].rearrange("(c p) n -> p c n", p=P)).then_inc(ld_raw, 16)

        raw_weights(0)
        sp.wait_ge(c["lgc"], C + NT)
        sp.dma_start(b2r[:, :], b2_rows.rearrange("r e f -> r (e f)")).then_inc(ld["b1r"], 16)

        def load_shared(i, par):
            sp.wait_ge(f["xT"], C + i - 1)
            sp.dma_start(xf_sb[par][:, :], XN3[:, bass.ds(i, 1), :].rearrange("p t d -> p (t d)")).then_inc(f_x[par], 16)

        sp.wait_ge(c["x3c"], C + NT)
        with sp.Fori(0, NT // 2) as j:
            load_shared(j * 2, 0)
            load_shared(j * 2 + 1, 1)

        raw_weights(1)
        sp.wait_ge(scattered, 16 * 2 * NT)
        sp.wait_ge(rt_done, 1)
        pairs = sp.value_load(ends[0:1, E:E + 1], min_val=NT, max_val=BLOCKS // 2)

        def slots(i, par, on):
            if on[0]:
                sp.wait_ge(f["xT"], C + i - 1)
                sp.dma_start(xf_sb[par][:, :], slot_tiles[bass.ds(i - NT, 1)].rearrange("t p d -> p (t d)")).then_inc(f_x[par], 16)
            if on[2]:
                sp.wait_ge(f["y"], C + i - 1)
                sp.dma_start(slot_out[bass.ds(i - 2 - NT, 1)].rearrange("t p d -> p (t d)"), y_sb[par][:, :]).then_inc(f_st[par], 16)

        sweep(sp, NT, pairs, slots)

        sp.wait_ge(g_done, 16 * NT)

    @block.gpsimd
    def _(pool):
        for s in credited:
            pool.sem_inc(s, C)
        steps = 0

        def did(ins):
            nonlocal steps
            steps += 1
            ins.then_inc(made_steps, 1)

        pool.memset(zeros[:, :], 0.0).then_inc(z_made, 1)
        pool.wait_ge(z_made, 1)
        did(pool.memset(ident[:, :], 0.0))
        did(pool.memset(identb[:, :], 0.0))
        did(pool.memset(ones[:, :], 1.0))
        did(pool.memset(onesb[:, :], 1.0))
        did(pool.memset(before[:, :], 1.0))
        did(pool.memset(minus_half[:, :], -0.5))
        did(pool.memset(window[:, :], 0.0))
        did(pool.memset(qs[:, :, :], 0.0))
        did(pool.memset(ks[:, :, :], 0.0))
        did(pool.memset(lastk[:, :, :], 0.0))
        did(pool.memset(vinit[:, :, :], 0.0))
        did(pool.memset(wo_pad[:, :, :, :], 0.0))
        pool.wait_ge(made_steps, steps)
        for m in (ident, identb):
            did(pool.affine_select(out=m[:, :], in_=m[:, :], compare_op=ALU.not_equal, fill=1.0,
                                   base=0, pattern=[[-1, P]], channel_multiplier=1))
        did(pool.affine_select(out=before[:, :], in_=before[:, :], compare_op=ALU.is_gt, fill=0.0,
                               base=0, pattern=[[1, P]], channel_multiplier=-1))
        owns = window[:, 0:P], window[:, P + 2 * W:]
        prev = window[:, P:P + 2 * W].rearrange("p (n w) -> p n w", n=2)
        for own in owns:
            did(pool.affine_select(out=own, in_=own, compare_op=ALU.is_ge, fill=MASKED, base=0,
                                   pattern=[[-1, P]], channel_multiplier=1))
        did(pool.affine_select(out=prev, in_=prev, compare_op=ALU.is_ge, fill=MASKED, base=-1,
                               pattern=[[0, 2], [1, W]], channel_multiplier=-1))
        pool.wait_ge(made_steps, steps)
        for own in owns:
            did(pool.affine_select(out=own, in_=own, compare_op=ALU.is_ge, fill=MASKED, base=W - 1,
                                   pattern=[[1, P]], channel_multiplier=-1))
        pool.wait_ge(made_steps, steps)
        pool.wait_ge(ks_hi, 1)
        pool.tensor_copy(ks[0:W, :, 32:48], ks[0:W, :, 0:16]).then_inc(ks_dup, 1)
        pool.wait_ge(ld["lastv"], 32)
        pool.sem_inc(made, 1)
        bias_steps = 0

        def step(ins):
            nonlocal bias_steps
            bias_steps += 1
            ins.then_inc(p_steps, 1)
            pool.wait_ge(p_steps, bias_steps)

        pool.wait_ge(ld["bias"], 80)
        for whole, parts in ((bias1, bias1p), (bias2, bias2p)):
            step(pool.tensor_copy(parts[:, 0, :], whole[:, :]))
            pool.sem_inc(bias_split, 1)
            step(pool.tensor_tensor(whole[:, :], whole[:, :], parts[:, 0, :], ALU.subtract))
            step(pool.tensor_copy(parts[:, 1, :], whole[:, :]))
            pool.sem_inc(bias_split, 1)
            step(pool.tensor_tensor(whole[:, :], whole[:, :], parts[:, 1, :], ALU.subtract))
            step(pool.tensor_copy(parts[:, 2, :], whole[:, :]))
            pool.sem_inc(bias_split, 1)
        pool.wait_ge(p_pe, CHUNKS)
        pool.wait_ge(p_act, CHUNKS)
        pool.wait_ge(ks_dup, 1)
        for i in range(2):
            pool.memset(qe[i][64:P, :, :].bitcast(F32), 0.0).then_inc(made, 1)
        pool.wait_ge(made, 3)

        def inverse_deviation(st, s, t):
            pool.wait_ge(s, C + t * 4 + 3)
            pool.tensor_tensor(st[:, 8:9], st[:, 7:8], minus_half[:, :], ALU.pow).then_inc(s, 1)

        with pool.Fori(0, NT) as t:
            inverse_deviation(stats, a["ln"], t)

        def split_weights(g):
            if g < PLACES:
                pool.wait_ge(ld_raw, 32 * (g + 1))
            else:
                pool.wait_ge(ld_raw_pool, 32 * (g - PLACES + 1))
            high, low = wts[:, g % PLACES, 0, :], wts[:, g % PLACES, 1, :]
            pool.tensor_copy(high, raw[:, :]).then_inc(w_split, 1)
            pool.wait_ge(w_split, 2 * g + 1)
            pool.tensor_tensor(low, raw[:, :], high.bitcast(F32), ALU.subtract).then_inc(w_split, 1)

        pool.wait_ge(a["x1"], C + NT)
        pool.wait_ge(ld_raw, 32)

        def cross(i, par, on):
            if on[3]:
                inverse_deviation(stats3, c["ln3"], i - 3)
            if on[0]:
                inverse_deviation(stats2, c["ln"], i)
            if on[1]:
                t = i - 1
                pool.wait_ge(c["xn"], C + t + 1)
                xt = X[:, bass.ds(t, 1), :].rearrange("p t d -> p (t d)")
                pool.tensor_tensor(xt, xt, b_out[:, :], ALU.add).then_inc(c["bo"], 1)
                part = bass.ds(t * (WN // NT), WN // NT)
                high, low = wts[:, 0, 0, part], wts[:, 0, 1, part]
                pool.tensor_copy(high, raw[:, part]).then_inc(c["wh"], 1)
                pool.wait_ge(c["wh"], C + t + 1)
                pool.tensor_tensor(low, raw[:, part], high.bitcast(F32), ALU.subtract).then_inc(c["wl"], 1)
            if on[1]:
                pool.wait_ge(c["rd"], C + t + 1)
                pr = prob2[1 - par][:, :, :]
                pool.tensor_tensor(pr, pr, den2[:, 1, :].unsqueeze(2).broadcast_to([P, XH, CK]), ALU.mult).then_inc(c["nrm"], 1)

        sweep(pool, 0, NT // 2, cross, 4)
        pool.wait_ge(c["wl"], C + NT)
        pool.sem_inc(w_split, 2)
        pool.wait_ge(c["x2"], C + NT)
        pool.wait_ge(c["lgc"], C + NT)
        pool.iota(iota8[:, :], pattern=[[1, E]], base=0, channel_multiplier=0,
                  allow_small_or_imprecise_dtypes=True).then_inc(rt_idx, 1)
        pool.wait_ge(rt_idx, 1)
        pool.iota(iotab[:, :], pattern=[[1, BLOCKS]], base=0, channel_multiplier=0,
                  allow_small_or_imprecise_dtypes=True).then_inc(rt_idx, 1)
        pool.wait_ge(rt_idx, 2)
        split_weights(1)
        pool.wait_ge(zeroed, 16 * (2 * BLOCKS - 2 * NT))
        pool.wait_ge(rt_done, 1)
        for t in range(NT):
            for k in range(2):
                pool.indirect_dma_start(slot_x, bass.IndirectOffsetOnAxis(dest[:, k, t:t + 1], 0),
                                        XN3[:, t, :], None).then_inc(scattered, 16)
        def load_weights(g):
            pool.wait_ge(w_split, 2 * g)
            pool.dma_start(raw[:, 0:DC * FF].rearrange("p (c f) -> p c f", c=DC),
                           ew1[g - 1].rearrange("(c p) f -> p c f", p=P)).then_inc(ld_raw_pool, 16)
            pool.dma_start(raw[:, DC * FF:].rearrange("p (c n) -> p c n", c=KF),
                           ew2[g - 1].rearrange("(c p) n -> p c n", p=P)).then_inc(ld_raw_pool, 16)

        split_weights(2)
        load_weights(PLACES)
        for g in range(PLACES, E + 1):
            if g > PLACES:
                e = pool.value_load(ends[0:1, g - PLACES - 1:g - PLACES], min_val=0, max_val=BLOCKS)
                pool.wait_ge(f["dn"], e + (C + NT))
                pass_waits(pool)
            else:
                pool.wait_ge(f["dn"], C + NT)
            split_weights(g)
            if g < E:
                load_weights(g + 1)

        pairs = pool.value_load(ends[0:1, E:E + 1], min_val=NT, max_val=BLOCKS // 2)
        pool.wait_ge(f_st[0], pairs * 16 + C)
        pool.wait_ge(f_st[1], pairs * 16 + C)
        pass_waits(pool)
        for t in range(NT):
            for k, y in enumerate((ya, yb)):
                pool.indirect_dma_start(y[:, t, :], None, slot_y,
                                        bass.IndirectOffsetOnAxis(dest[:, k, t:t + 1], 0)).then_inc(g_y[t], 16)

    self_qkv, self_s, self_t = PQ[0], PQ[1], PQ[2]
    self_o = PQ[3][:, 0, :].rearrange("p (g n) -> p g n", g=HG)
    self_m = PQ[3][:, 1, :]
    BANKS = ((PQ[0][:, 0, :], 0, 6), (PQ[0][:, 1, :], 6, 12), (PQ[1][:, 0, :], 12, XH))
    cross_x = PQ[1][:, 1, 0:D]
    cross_t = (PQ[2][:, 0, :], PQ[2][:, 1, :], PQ[3][:, 0, :])
    TCH = ((0, 4), (4, 8), (8, FC))
    cross_o = PQ[3][:, 1, 0:D]
    cross_l = PQ[1][:, 0, 512 - E:512]
    cross_x3 = PQ[3][:, 0, D:2 * D]
    up_banks = (PQ[0], PQ[3])
    down_t = PQ[1]
    down_y = PQ[2][:, 0, 0:D]
    ffn_x = PQ[2][:, 1, 0:D]

    def tile_of(t):
        return X[:, bass.ds(t, 1), :].rearrange("p t d -> p (t d)")

    def sweep_self_attention(eng, body):
        for k in range(2):
            body(k, k, [n <= k for n in range(3)] + [True])
        for b in range(B):
            with eng.Fori(b * TB // 2 + 1, (b + 1) * TB // 2 - (b + 1) // B) as j:
                body(j * 2, 0, [True] * 4)
                body(j * 2 + 1, 1, [True] * 4)
            if b + 1 < B:
                for k in range(2):
                    body((b + 1) * TB + k, k, [True] * 4, b + 1)
        for k in range(2):
            body(NT - 2 + k, k, [True] * 3 + [k == 0])
        for k in range(2):
            body(NT + k, k, [n > k for n in range(3)] + [False])

    def before_of(stack):
        places = stack[:, :, :].rearrange("p c (n w) -> p c n w", w=W)
        return places[:, :, 0:4:3, :]

    def twice(keys):
        return keys.unsqueeze(2).broadcast_to([P, keys.shape[1], 2, W])

    def unit(i, par, on, w):
        return C + (i - 1) * 8 + w, on[1] if w >= 0 else on[2], 1 - par if w >= 0 else par

    @block.tensor
    def _(pe):
        def begins(n):
            if n >= 4:
                pe.wait_ge(p_act, n - 3)
                pe.wait_ge(p_dve, n - 3)
            return PQ[n % 4]

        pe.wait_ge(made_steps, 15)
        pe.wait_ge(ld["w4"], 64)
        for ch in range(DC):
            ps = begins(CH_WT + ch)
            for n in range(3):
                for r in range(DC):
                    last = pe.transpose(ps[:, n // 2, n % 2 * D + r * P:n % 2 * D + (r + 1) * P],
                                        w4[:, n, r, ch * P:(ch + 1) * P], ident[:, :])
            last.then_inc(p_pe, 1)
        pe.wait_ge(wo_padded, 1)
        ps = begins(CH_WO)
        for g in range(HG):
            for r in range(DC):
                last = pe.transpose(ps[:, g // 2, g % 2 * D + r * P:g % 2 * D + (r + 1) * P],
                                    wo_pad[:, r, 4 * g:4 * g + 4, :].rearrange("p h k -> p (h k)"), ident[:, :])
        last.then_inc(p_pe, 1)
        pe.wait_ge(ld["ctx"], 16)
        ps = begins(CH_CT)
        for b in range(B):
            pe.transpose(ps[:, 0, b * CK:(b + 1) * CK], ctx_sb[:, b, 0:P], ident[0:CK, 0:CK])
            last = pe.transpose(ps[0:CD - P, 1, b * CK:(b + 1) * CK], ctx_sb[:, b, P:CD], ident[0:CK, 0:CK])
        last.then_inc(p_pe, 1)
        pe.wait_ge(ks_dup, 1)
        pe.wait_ge(ks_lo, 1)
        ps = begins(CH_KI)
        for p in range(H // 2):
            last = pe.transpose(ps[:, p // 4, p % 4 * W:(p % 4 + 1) * W],
                                ks[0:W, 2 * p:2 * p + 2, :].rearrange("p h k -> p (h k)"), ident[0:W, 0:W])
        last.then_inc(p_pe, 1)
        pe.wait_ge(ld["xq"], 16)
        for ch in range(2):
            ps = begins(CH_WQ + ch)
            for p in range(4):
                for r in range(DC):
                    last = pe.transpose(ps[:, p // 2, p % 2 * D + r * P:p % 2 * D + (r + 1) * P],
                                        xq_sb[:, r, (4 * ch + p) * P:(4 * ch + p + 1) * P], ident[:, :])
            last.then_inc(p_pe, 1)
        pe.wait_ge(p_act, CH_CT + 1)
        pe.wait_ge(p_dve, CH_CT + 1)
        for first, w_sb, s in ((CH_K, xk_sb, "xk"), (CH_V, xv_sb, "xv")):
            pe.wait_ge(ld[s], 32)
            for ch in range(2):
                ps = begins(first + ch)
                for p in range(4):
                    o = ps[:, p // 2, p % 2 * B * CK:(p % 2 + 1) * B * CK]
                    at = (4 * ch + p) * P
                    pe.matmul(o, w_sb[:, 0, at:at + P], cT[:, 0, :], start=True, stop=False)
                    last = pe.matmul(o, w_sb[0:CD - P, 1, at:at + P], cT[0:CD - P, 1, :], start=False, stop=True)
                last.then_inc(p_pe, 1)
        pe.wait_ge(p_act, CH_K + 2)
        pe.wait_ge(p_dve, CH_K + 2)
        for n in range(8):
            b, ch, half = n // 4, n // 2 % 2, n % 2
            ps = begins(CH_A + n)
            for p in range(4):
                last = pe.matmul(ps[:, p // 2, p % 2 * 2 * CK:(p % 2 + 1) * 2 * CK],
                                 wqT[:, 4 * half + p, ch * P:(ch + 1) * P], KB[:, b, 4 * half + p, :],
                                 start=True, stop=True)
            last.then_inc(p_pe, 1)
        pe.wait_ge(ld["xo"], 16)
        pe.wait_ge(p_act, CH_V + 2)
        pe.wait_ge(p_dve, CH_V + 2)
        for n, (b, c0) in enumerate(VW_CH):
            ps = begins(CH_VW + n)
            for ch in range(c0, min(c0 + 4, FC)):
                M = vw_rows(ch)
                o = ps[0:M, (ch - c0) // 2, (ch - c0) % 2 * D:((ch - c0) % 2 + 1) * D]
                over = [p for p in range(HP) if 2 * CK * p < ch * P + M and 2 * CK * (p + 1) > ch * P]
                for p in over:
                    at = P + ch * P - 2 * CK * p
                    last = pe.matmul(o, VB[:, p, b, at:at + M], xo_sb[:, p, :],
                                     start=p == over[0], stop=p == over[-1])
            last.then_inc(p_pe, 1)

        pe.wait_ge(p_act, CHUNKS)
        pe.wait_ge(p_dve, CHUNKS)
        pe.wait_ge(made, 3)
        pe.wait_ge(v_made, 6)

        def self_attention(i, par, on, starts=0):
            def scores(u):
                if u == 0:
                    for s in ("qE", "qO", "kA", "kD"):
                        pe.wait_ge(a[s], C + i)
                    for s in ("pA", "pD"):
                        pe.wait_ge(a[s], C + i - 1)
                    if starts and par:
                        pe.wait_ge(a_k0, starts + 1)
                n = unit(i, par, on, u)[0]
                pe.wait_ge(a["exp"], n - 1)
                ps = self_s[:, u % 2, 0:2 * KW]
                pe.matmul(ps, identb[:, :], window[:, :], start=True, stop=False)
                pe.matmul(ps[:, 0:KW], qe[1 - par][:, u, :], kst[1 - par][:, u, W:W + KW], start=False, stop=False)
                pe.matmul(ps[:, KW:2 * KW], qo[1 - par][:, u, :], kst[1 - par][:, u, 0:KW],
                          start=False, stop=True).then_inc(a["S"], 1)

            def transposed(w):
                n, is_on, _ = unit(i, par, on, w)
                if not is_on:
                    return
                pe.wait_ge(a["exp"], n + 1)
                pe.wait_ge(a[f"ev{w % 2}"], C + (i - 1) * 4 + w // 2)
                for k in range(3):
                    last = pe.transpose(self_t[:, w % 2, k * P:(k + 1) * P], prob[w % 4][:, k * P:(k + 1) * P], ident[:, :])
                last.then_inc(a["tr"], 1)

            def output(w):
                _, is_on, side = unit(i, par, on, w)
                if not is_on:
                    return
                pe.wait_ge(a[f"ev{w % 2}"], C + (i - 1) * 4 + w // 2 + 1)
                if w == 0:
                    pe.wait_ge(a["on"], C + i - 1)
                    pe.wait_ge(a["v"], C + i)
                    pe.wait_ge(a_vp[1 - par], (i + par) * 16 + C)
                at = w % 8
                rows, g = at % 2 * 2 * HROW, at // 2
                for n in range(2):
                    o = self_o[rows + n * HROW:rows + (n + 1) * HROW, g, :]
                    pe.matmul(o, V[side][:, 2 * at + n, :], pt[w % 2][:, 2 * n, :], start=True, stop=False)
                pe.matmul(self_o[rows:rows + 2 * HROW, g, :],
                          vprev[side][:, 2 * at:2 * at + 2, :].rearrange("p h v -> p (h v)"),
                          pt[w % 2][:, 1, :], start=False, stop=True).then_inc(a["pv"], 1)

            for u in range(8):
                if on[1] and u > 0:
                    scores(u)
                transposed(u - 2)
                if u == 0:
                    output(u - 3)
                if on[1] and u == 0:
                    scores(u)
                if on[0] and u == 0:
                    pe.wait_ge(a["xn"], C + i + 1)
                    pe.wait_ge(a["pA"], C + i)
                    pe.wait_ge(a["pD"], C + i)
                    for ch in range(DC):
                        last = pe.transpose(self_qkv[:, 0, ch * P:(ch + 1) * P], xn[:, ch * P:(ch + 1) * P], ident[:, :])
                    last.then_inc(a["xT"], 1)
                if on[2] and u == 1:
                    pe.wait_ge(a["rd"], C + i - 1)
                    pe.wait_ge(a["x1"], C + i - 2)
                    for g in range(HG):
                        last = pe.transpose(self_m[:, g * P:(g + 1) * P],
                                            rden[:, 4 * g:4 * g + 4, :].rearrange("p h k -> p (h k)"), ident[:, :])
                    last.then_inc(a["rT"], 1)
                if on[0] and u == 2:
                    pe.wait_ge(a["xh"], C + i + 1)
                    pe.wait_ge(a["xl"], C + i + 1)
                    for o, lo, hi in ((self_qkv[:, 0, :], 0, 2 * D), (self_qkv[:, 1, 0:D], 2 * D, 3 * D)):
                        for ch in range(DC):
                            last = split_product(pe, o, (xth[:, ch, :], xtl[:, ch, :]),
                                                 (WTh[:, ch, lo:hi], WTl[:, ch, lo:hi]), ch == 0, ch == 1)
                    last.then_inc(a["qkv"], 1)
                if on[2] and u == 5:
                    pe.wait_ge(a["oh"], C + i - 1)
                    pe.wait_ge(a["ol"], C + i - 1)
                    for g in range(HG):
                        last = split_product(pe, self_m[:, 0:D], (oth[:, g, :], otl[:, g, :]),
                                             (WOh[:, g, :], WOl[:, g, :]), g == 0, g == HG - 1)
                    last.then_inc(a["op"], 1)
                if on[0] and u == 4:
                    pe.wait_ge(a["lo"], C + i + 1)
                    pe.wait_ge(a["v"], C + i + 1)
                    for p in range(H // 2):
                        last = pe.transpose(self_qkv[:, p // 4, p % 4 * P:(p % 4 + 1) * P],
                                            qs[:, 2 * p:2 * p + 2, :].rearrange("p h k -> p (h k)"), ident[:, :])
                    last.then_inc(a["qT"], 1)
                if on[0] and u == 6:
                    pe.wait_ge(a["qE"], C + i + 1)
                    pe.wait_ge(a["qO"], C + i + 1)
                    for p in range(H // 2):
                        last = pe.transpose(self_qkv[:, p // 4, p % 4 * P:(p % 4 + 1) * P],
                                            ks[:, 2 * p:2 * p + 2, :].rearrange("p h k -> p (h k)"), ident[:, :])
                    last.then_inc(a["kT"], 1)
                if u > 0:
                    output(u - 3)

        pe.wait_ge(a_k0, 1)
        sweep_self_attention(pe, self_attention)

        pe.wait_ge(a["x1"], C + NT)

        def cross(i, par, on):
            if on[1]:
                batch = bass.ds((i - 1) // TB, 1)
                pe.wait_ge(c["xh"], C + i)
                pe.wait_ge(c["xl"], C + i)
                for k, (ps, h0, h1) in enumerate(BANKS):
                    if k == 0:
                        pe.wait_ge(c["exp"], C + (i - 2) * 2 + 1)
                    else:
                        pe.wait_ge(c["sub"], C + (i - 2) * 2 + k)
                    if k == 2:
                        pe.wait_ge(c["lgc"], C + i - 3)
                    for ch in range(DC):
                        right = [m[:, batch, ch, h0 * CK:h1 * CK].rearrange("p b n -> p (b n)") for m in (Ah, Al)]
                        last = split_product(pe, ps[:, 0:(h1 - h0) * CK], (xt2h[:, ch, :], xt2l[:, ch, :]),
                                             right, ch == 0, ch == 1)
                    last.then_inc(c["S"], 1)
            if on[0]:
                pe.wait_ge(c["xn"], C + i + 1)
                pe.wait_ge(c["xl"], C + i)
                for ch in range(DC):
                    last = pe.transpose(cross_x[:, ch * P:(ch + 1) * P], xn2[:, ch * P:(ch + 1) * P], ident[:, :])
                last.then_inc(c["xT"], 1)
            if on[3]:
                pe.wait_ge(c["xn3"], C + i - 2)
                pe.wait_ge(c["pl"], C + (i - 2) * 3)
                for ch in range(DC):
                    last = pe.transpose(cross_x3[:, ch * P:(ch + 1) * P],
                                        XN3c[:, ch * P:(ch + 1) * P], ident[:, :])
                last.then_inc(c["x3T"], 1)
            if on[2]:
                pe.wait_ge(c["nrm"], C + i - 1)
                flat = prob2[par][:, :, :].rearrange("p h k -> p (h k)")
                for k, (c0, c1) in enumerate(TCH):
                    pe.wait_ge(c["pl"], C + (i - 3) * 3 + k + 1)
                    if k == 2 and on[3]:
                        pe.wait_ge(c["x3"], C + i - 2)
                    for n in range(c0, c1):
                        M = vw_rows(n)
                        last = pe.transpose(cross_t[k][0:M, (n - c0) * P:(n - c0 + 1) * P], flat[:, n * P:n * P + M], ident[:, :])
                    last.then_inc(c["pT"], 1)
            if on[3]:
                pe.wait_ge(c["x3"], C + i - 2)
                if on[1]:
                    pe.wait_ge(c["sub"], C + i * 2)
                pe.wait_ge(c["lgc"], C + i - 3)
                pe.matmul(cross_l, ones[0:1, :], rb_sb[:, :], start=True, stop=False)
                for ch in range(DC):
                    last = pe.matmul(cross_l, x3t[:, ch, :], rw_sb[:, ch, :], start=False, stop=ch == 1)
                last.then_inc(c["lg"], 1)
            if on[2]:
                batch = bass.ds((i - 2) // TB, 1)
                pe.wait_ge(c["x2"], C + i - 2)
                for k, (c0, c1) in enumerate(TCH):
                    pe.wait_ge(c["pl"], C + (i - 2) * 3 + k + 1)
                    for n in range(c0, c1):
                        M = vw_rows(n)
                        right = [m[0:M, batch, n, :].rearrange("p b d -> p (b d)") for m in (VWh, VWl)]
                        last = split_product(pe, cross_o, (pth[0:M, n, :], ptl[0:M, n, :]), right, n == 0, n == FC - 1)
                last.then_inc(c["o"], 1)

        pe.wait_ge(ld["small"], 48)
        sweep(pe, 0, NT // 2, cross, 4)

        pe.wait_ge(rt, RT_SEL)
        pe.matmul(rank_ps, before[:, :], sel.rearrange("p t e -> p (t e)"), start=True, stop=True).then_inc(rt_pe, 1)
        pe.matmul(total_ps, ones[:, :], sel.rearrange("p t e -> p (t e)"), start=True, stop=True).then_inc(rt_pe, 1)

        def experts(routed):
            def body(i, par, on):
                def weights_of(block, rows):
                    if not routed:
                        return (lambda part, lo, n: wts[:, 0, part, lo:lo + n]), (lambda n, at: rows[0:3, at:at + n])
                    width = FF if rows is b1r else D
                    at_block = bass.ds(block - NT, 1)
                    stage = pe.value_load(stage_of[0:1, at_block], min_val=1, max_val=E)
                    place = pe.value_load(place_of[0:1, at_block], min_val=0, max_val=PLACES - 1)
                    if rows is b1r:
                        pe.wait_ge(w_split, stage * 2 + 2)
                    return (lambda part, lo, n: wts[:, bass.ds(place, 1), part, lo:lo + n].rearrange("p o n -> p (o n)"),
                            lambda n, at: rows[0:3, bass.ds(stage * width + at, n)])

                if on[1]:
                    weight, bias = weights_of(i - 1, b1r)
                    pe.wait_ge(f["xh"], C + i)
                    pe.wait_ge(f["xl"], C + i)
                    pe.wait_ge(f["act"], C + i - 2)
                    ps = up_banks[1 - par]
                    for n in range(2):
                        pe.matmul(ps[:, n, :], onesb[0:3, :], bias(512, n * 512), start=True, stop=False)
                    for ch in range(DC):
                        for part in range(2):
                            for n in range(2):
                                pe.matmul(ps[:, n, :], fxh[:, ch, :], weight(part, ch * FF + n * 512, 512), start=False, stop=False)
                        for n in range(2):
                            last = pe.matmul(ps[:, n, :], fxl[:, ch, :], weight(0, ch * FF + n * 512, 512), start=False, stop=ch == 1)
                    last.then_inc(f["up"], 1)
                if on[0]:
                    pe.wait_ge(f_x[par], (i - par) * 8 + 16)
                    pe.wait_ge(f["xl"], C + i)
                    for ch in range(DC):
                        last = pe.transpose(ffn_x[:, ch * P:(ch + 1) * P], xf_sb[par][:, ch * P:(ch + 1) * P], ident[:, :])
                    last.then_inc(f["xT"], 1)
                if on[2]:
                    weight, bias = weights_of(i - 2, b2r)
                    pe.wait_ge(f["hl"], C + (i - 1) * 2)
                    pe.wait_ge(f["y"], C + i - 2)
                    pe.matmul(down_y, onesb[0:3, :], bias(D, 0), start=True, stop=False)
                    for k in range(KF):
                        last = split_product(pe, down_y, (hth[:, k, :], htl[:, k, :]),
                                             [weight(part, DC * FF + k * D, D) for part in range(2)], False, k == KF - 1)
                    last.then_inc(f["dn"], 1)
                if on[1]:
                    pe.wait_ge(f["act"], C + i)
                    pe.wait_ge(f["hl"], C + (i - 1) * 2)
                    for n in range(2):
                        for k in range(4):
                            last = pe.transpose(down_t[:, n, k * P:(k + 1) * P], hact[:, (4 * n + k) * P:(4 * n + k + 1) * P], ident[:, :])
                        last.then_inc(f["hT"], 1)
            return body

        pe.wait_ge(ld["b1r"], 32)
        pe.wait_ge(w_split, 2)
        sweep(pe, 0, NT // 2, experts(False))
        pe.wait_ge(rt_done, 1)
        pairs = pe.value_load(ends[0:1, E:E + 1], min_val=NT, max_val=BLOCKS // 2)
        sweep(pe, NT, pairs, experts(True))

    @block.scalar
    def _(act):
        def copy(o, i, scale=1.0):
            return nc.scalar.activation(o, i, ACT.Copy, scale=scale)

        act.dma_start(bias1[0:1, :], sb1.rearrange("(o n) -> o n", o=1)).then_inc(ld["bias"], 16)
        act.dma_start(bias1[1:E + 1, :], eb1).then_inc(ld["bias"], 16)
        act.dma_start(bias2[0:1, :], sb2.rearrange("(o n) -> o n", o=1)).then_inc(ld["bias"], 16)
        act.dma_start(bias2[1:E + 1, :], eb2).then_inc(ld["bias"], 16)
        act.dma_start(bias2[E + 1:E + 2, :], xb.rearrange("(o n) -> o n", o=1)).then_inc(ld["bias"], 16)
        act.dma_start(rw_sb[:, :, :], rw.rearrange("(c p) e -> p c e", p=P)).then_inc(ld["small"], 16)
        act.dma_start(rb_sb[:, :], rb.rearrange("(o n) -> o n", o=1)).then_inc(ld["small"], 16)
        act.dma_start(b_out[:, :], xb.rearrange("(o n) -> o n", o=1).broadcast_to([P, D])).then_inc(ld["small"], 16)
        act.wait_ge(made_steps, 15)
        act.wait_ge(ld["last"], 16)
        copy(ks[0:W, :, 0:16].bitcast(F32R), lastk[:, :, :]).then_inc(ks_hi, 1)
        for ch in range(DC):
            act.wait_ge(p_pe, CH_WT + ch + 1)
            copy(WTh[:, ch, :], PQ[CH_WT + ch][:, :, :].rearrange("p a n -> p (a n)")[:, 0:3 * D]).then_inc(p_act, 1)
        act.wait_ge(p_pe, CH_WO + 1)
        copy(WOh[:, :, :].rearrange("p (a g) n -> p a (g n)", a=2), PQ[CH_WO][:, :, :]).then_inc(p_act, 1)
        act.wait_ge(p_pe, CH_CT + 1)
        copy(cT[:, 0, :], PQ[CH_CT % 4][:, 0, 0:B * CK]).then_inc(p_act, 1)
        act.wait_ge(p_pe, CH_KI + 1)
        copy(kinit[:, 0:4, :], PQ[CH_KI % 4][:, 0, 0:4 * W].rearrange("p (a w) -> p a w", a=4)).then_inc(p_act, 1)
        for ch in range(2):
            act.wait_ge(p_pe, CH_WQ + ch + 1)
            copy(wqT[:, 4 * ch:4 * ch + 2, :], PQ[(CH_WQ + ch) % 4][:, 0, :].rearrange("p (a d) -> p a d", a=2)).then_inc(p_act, 1)
        act.wait_ge(kv_made, 2)
        for first in (CH_K, CH_V):
            for ch in range(2):
                act.wait_ge(p_pe, first + ch + 1)
                for q in range(2):
                    for r in range(2):
                        half = slice(r * XD, (r + 1) * XD)
                        src = PQ[(first + ch) % 4][half, 0, q * B * CK:(q + 1) * B * CK].rearrange("p (b k) -> p b k", b=B)
                        p = 4 * ch + q
                        if first == CH_K:
                            last = copy(KB[half, :, p, r * CK:(r + 1) * CK], src, XD ** -0.5)
                        else:
                            last = copy(VB[half, p, :, P + r * CK:P + (r + 1) * CK], src)
                last.then_inc(p_act, 1)
        for n in range(8):
            b, ch, half = n // 4, n // 2 % 2, n % 2
            act.wait_ge(p_pe, CH_A + n + 1)
            copy(Ah[:, b, ch, half * HALF:(half + 1) * HALF].rearrange("p (a n) -> p a n", a=2),
                 PQ[(CH_A + n) % 4][:, :, 0:HALF // 2]).then_inc(p_act, 1)
        for n, (b, c0) in enumerate(VW_CH):
            act.wait_ge(p_pe, CH_VW + n + 1)
            ps = PQ[(CH_VW + n) % 4]
            if c0 + 4 <= FC:
                last = copy(VWh[:, b, c0:c0 + 4, :].rearrange("p (a c) d -> p a (c d)", a=2), ps[:, :, :])
            else:
                copy(VWh[:, b, c0, :], ps[:, 0, 0:D])
                last = copy(VWh[0:FLAST, b, c0 + 1, :], ps[0:FLAST, 0, D:2 * D])
            last.then_inc(p_act, 1)

        act.wait_ge(p_pe, CHUNKS)
        act.wait_ge(made, 3)
        act.wait_ge(v_made, 6)

        def self_attention(i, par, on, starts=0):
            keys = self_qkv[:, 0, :].rearrange("p (c n) -> p c n", c=4)
            for u in range(8):
                w = u - 2
                n, is_on, _ = unit(i, par, on, w)
                if is_on and w % 2:
                    act.wait_ge(a["tr"], n + 1)
                    act.wait_ge(a["pv"], n - 1)
                    copy(pt[1][:, :, :], self_t[:, 1, 0:3 * P].rearrange("p (a n) -> p a n", a=3)).then_inc(a["ev1"], 1)
                if on[1] and u == 0:
                    act.wait_ge(a["S"], C + (i - 1) * 8)
                    copy(before_of(kst[par])[:, 0:4], twice(keys[:, :, P - W:P])).then_inc(a["pA"], 1)
                if on[0] and u == 0:
                    act.wait_ge(a["xT"], C + i + 1)
                    copy(xth[:, :, :], self_qkv[:, 0, 0:D].rearrange("p (c n) -> p c n", c=DC)).then_inc(a["xh"], 1)
                if on[2] and u == 2:
                    act.wait_ge(a["rT"], C + i - 1)
                    act.wait_ge(a["ol"], C + i - 2)
                    copy(o_sb[:, :, :], self_m.rearrange("p (g n) -> p g n", g=HG)).then_inc(a["rS"], 1)
                if on[2] and u == 4:
                    act.wait_ge(a["on"], C + i - 1)
                    act.wait_ge(a["op"], C + i - 2)
                    copy(oth[:, :, :], o_sb[:, :, :]).then_inc(a["oh"], 1)
                if on[0] and u == 3:
                    act.wait_ge(a["qkv"], C + i + 1)
                    for m, at, scale in ((qs[:, :, 0:32], 0, DH ** -0.5), (ks[:, :, :], D, 1.0)):
                        places = m.rearrange("p h (c k) -> p h c k", c=2)[:, :, :, 0:16]
                        src = self_qkv[:, 0, at:at + D].rearrange("p (h d) -> p h d", h=H)
                        last = copy(places.bitcast(F32R), src.unsqueeze(2).broadcast_to([P, H, 2, DH]), scale)
                    last.then_inc(a["hi"], 1)
                if on[0] and u == 5:
                    act.wait_ge(a["qT"], C + i + 1)
                    copy(qe[par][0:64, :, :].rearrange("p (a c) n -> p a (c n)", a=2), self_qkv[0:64, :, :]).then_inc(a["qE"], 1)
                if on[1]:
                    n, _, _ = unit(i, par, on, u)
                    act.wait_ge(a["max"], n + 1)
                    act.wait_ge(a["tr"], n - 3)
                    if u == 0:
                        act.wait_ge(a["rd"], C + i - 2)
                    for k in range(2):
                        h = 2 * u + k
                        last = nc.scalar.activation(prob[u % 4][:, k * KW:(k + 1) * KW], self_s[:, u % 2, k * KW:(k + 1) * KW],
                                                    ACT.Exp, bias=negm[:, 1 - par, h:h + 1], accum_out=den[:, 1 - par, h:h + 1])
                    last.then_inc(a["exp"], 1)
                if on[0] and u == 7:
                    act.wait_ge(a["kT"], C + i + 1)
                    copy(kst[par][:, 0:4, W:KW], keys).then_inc(a["kA"], 1)

        sweep_self_attention(act, self_attention)

        act.wait_ge(a["x1"], C + NT)

        def cross(i, par, on):
            if on[0]:
                act.wait_ge(c["xT"], C + i + 1)
                copy(xt2h[:, :, :], cross_x.rearrange("p (c n) -> p c n", c=DC)).then_inc(c["xh"], 1)
            if on[3]:
                act.wait_ge(c["x3T"], C + i - 2)
                copy(x3t[:, :, :], cross_x3.rearrange("p (c n) -> p c n", c=DC)).then_inc(c["x3"], 1)
            if on[2]:
                for k, (c0, c1) in enumerate(TCH):
                    act.wait_ge(c["pT"], C + (i - 2) * 3 + k + 1)
                    if k < 2:
                        last = copy(pth[:, c0:c1, :], cross_t[k].rearrange("p (a n) -> p a n", a=4))
                    else:
                        copy(pth[:, c0, :], cross_t[k][:, 0:P])
                        last = copy(pth[0:FLAST, c0 + 1, :], cross_t[k][0:FLAST, P:2 * P])
                    last.then_inc(c["ph"], 1)
            if on[1]:
                act.wait_ge(c["nrm"], C + i - 2)
                act.wait_ge(c["pT"], C + (i - 2) * 3)
                act.wait_ge(c["max"], C + (i - 1) * 3 + 1)
                ps, h0, h1 = BANKS[0]
                for h in range(h0, h1):
                    last = nc.scalar.activation(prob2[1 - par][:, h, :], ps[:, h * CK:(h + 1) * CK], ACT.Exp,
                                                bias=negm2[:, h:h + 1], accum_out=den2[:, 0, h:h + 1])
                last.then_inc(c["exp"], 1)
                act.wait_ge(c["sub"], C + i * 2)
                rest = prob2[1 - par][:, h1:XH, :]
                nc.scalar.activation(rest, rest, ACT.Exp).then_inc(c["exp"], 1)

        sweep(act, 0, NT // 2, cross, 4)

        act.wait_ge(rt, RT_SHIFTED)
        nc.scalar.activation(e8[1][:, :, :], e8[0][:, :, :], ACT.Exp).then_inc(rt_act, 1)

        def experts(routed):
            def body(i, par, on):
                if on[1]:
                    act.wait_ge(f["up"], C + i)
                    act.wait_ge(f["hT"], C + (i - 1) * 2)
                    nc.scalar.activation(hact[:, :].rearrange("p (a n) -> p a n", a=2), up_banks[1 - par][:, :, :], ACT.Gelu).then_inc(f["act"], 1)
                if on[0]:
                    act.wait_ge(f["xT"], C + i + 1)
                    copy(fxh[:, :, :], ffn_x.rearrange("p (c n) -> p c n", c=DC)).then_inc(f["xh"], 1)
                if on[2] and routed:
                    act.wait_ge(f["dn"], C + i - 1)
                    act.wait_ge(f_st[par], (i - par - 2 - NT) * 8 + C)
                    copy(y_sb[par][:, :], down_y).then_inc(f["y"], 1)
                if on[1]:
                    for n in range(2):
                        act.wait_ge(f["hT"], C + (i - 1) * 2 + n + 1)
                        copy(hth[:, 4 * n:4 * n + 4, :], down_t[:, n, :].rearrange("p (a n) -> p a n", a=4)).then_inc(f["hh"], 1)
            return body

        sweep(act, 0, NT // 2, experts(False))
        act.wait_ge(rt_done, 1)
        pairs = act.value_load(ends[0:1, E:E + 1], min_val=NT, max_val=BLOCKS // 2)
        sweep(act, NT, pairs, experts(True))
        for t in range(NT):
            act.wait_ge(g_add, 2 * (t + 1))
            act.dma_start(of[:, t, :], X[:, t, :]).then_inc(g_done, 16)

    @block.vector
    def _(dve):
        def less_high(o, whole, high):
            return dve.tensor_tensor(o, whole, high.bitcast(F32), ALU.subtract)

        dve.memset(KB[:, :, :, :], 0.0).then_inc(kv_made, 1)
        dve.memset(VB[:, :, :, :], 0.0).then_inc(kv_made, 1)
        dve.wait_ge(ld["w4"], 64)
        dve.wait_ge(made_steps, 12)
        dve.tensor_copy(wo_pad[:, :, :, 0:DH], w4[:, 3, :, :].rearrange("p c (h d) -> p c h d", h=H)).then_inc(wo_padded, 1)
        dve.wait_ge(ks_hi, 1)
        less_high(ks[0:W, :, 16:32], lastk[:, :, :], ks[0:W, :, 0:16]).then_inc(ks_lo, 1)
        for ch in range(DC):
            dve.wait_ge(p_act, CH_WT + ch + 1)
            less_high(WTl[:, ch, :], PQ[CH_WT + ch][:, :, :].rearrange("p a n -> p (a n)")[:, 0:3 * D], WTh[:, ch, :]).then_inc(p_dve, 1)
        dve.wait_ge(p_act, CH_WO + 1)
        less_high(WOl[:, :, :].rearrange("p (a g) n -> p a (g n)", a=2), PQ[CH_WO][:, :, :],
                  WOh[:, :, :].rearrange("p (a g) n -> p a (g n)", a=2)).then_inc(p_dve, 1)
        dve.wait_ge(p_pe, CH_CT + 1)
        dve.tensor_copy(cT[0:CD - P, 1, :], PQ[CH_CT % 4][0:CD - P, 1, 0:B * CK]).then_inc(p_dve, 1)
        dve.wait_ge(p_pe, CH_KI + 1)
        dve.tensor_copy(kinit[:, 4:8, :], PQ[CH_KI % 4][:, 1, 0:4 * W].rearrange("p (a w) -> p a w", a=4)).then_inc(p_dve, 1)
        for ch in range(2):
            dve.wait_ge(p_pe, CH_WQ + ch + 1)
            dve.tensor_copy(wqT[:, 4 * ch + 2:4 * ch + 4, :], PQ[(CH_WQ + ch) % 4][:, 1, :].rearrange("p (a d) -> p a d", a=2)).then_inc(p_dve, 1)
        dve.wait_ge(kv_made, 2)
        for first in (CH_K, CH_V):
            for ch in range(2):
                dve.wait_ge(p_pe, first + ch + 1)
                for q in range(2):
                    for r in range(2):
                        half = slice(r * XD, (r + 1) * XD)
                        src = PQ[(first + ch) % 4][half, 1, q * B * CK:(q + 1) * B * CK].rearrange("p (b k) -> p b k", b=B)
                        p = 4 * ch + 2 + q
                        if first == CH_K:
                            last = dve.tensor_scalar(KB[half, :, p, r * CK:(r + 1) * CK], src, XD ** -0.5, None, ALU.mult)
                        else:
                            last = dve.tensor_copy(VB[half, p, :, P + r * CK:P + (r + 1) * CK], src)
                last.then_inc(p_dve, 1)
        for n in range(8):
            b, ch, half = n // 4, n // 2 % 2, n % 2
            cols = slice(half * HALF, (half + 1) * HALF)
            dve.wait_ge(p_act, CH_A + n + 1)
            less_high(Al[:, b, ch, cols].rearrange("p (a n) -> p a n", a=2), PQ[(CH_A + n) % 4][:, :, 0:HALF // 2],
                      Ah[:, b, ch, cols].rearrange("p (a n) -> p a n", a=2)).then_inc(p_dve, 1)
        dve.wait_ge(ld["brow"], 96)
        for n, (b, c0) in enumerate(VW_CH):
            dve.wait_ge(p_act, CH_VW + n + 1)
            ps = PQ[(CH_VW + n) % 4]
            if c0 + 4 <= FC:
                last = less_high(VWl[:, b, c0:c0 + 4, :].rearrange("p (a c) d -> p a (c d)", a=2), ps[:, :, :],
                                 VWh[:, b, c0:c0 + 4, :].rearrange("p (a c) d -> p a (c d)", a=2))
            else:
                less_high(VWl[:, b, c0, :], ps[:, 0, 0:D], VWh[:, b, c0, :])
                last = less_high(VWl[0:FLAST, b, c0 + 1, :], ps[0:FLAST, 0, D:2 * D], VWh[0:FLAST, b, c0 + 1, :])
            last.then_inc(p_dve, 1)

        def layer_norm_steps(o, tile, st, s, free):
            def moments(t):
                pass_waits(dve)
                dve.bn_stats(st[:, 0:6], tile(t)).then_inc(s, 1)

            def variance(t):
                dve.wait_ge(s, C + t * 4 + 1)
                pass_waits(dve)
                dve.bn_aggr(st[:, 6:8], st[:, 0:6]).then_inc(s, 1)
                dve.wait_ge(s, C + t * 4 + 2)
                dve.tensor_scalar(st[:, 7:8], st[:, 7:8], EPS, None, ALU.add).then_inc(s, 1)

            def normalized(t):
                dve.wait_ge(s, C + t * 4 + 4)
                dve.wait_ge(free, C + t)
                return dve.tensor_scalar(o, tile(t), st[:, 6:7], st[:, 8:9], ALU.subtract, ALU.mult)

            return moments, variance, normalized

        dve.wait_ge(p_pe, CHUNKS)
        dve.wait_ge(ld["x"], 16)
        moments, variance, normalized = layer_norm_steps(xn[:, :], tile_of, stats, a["ln"], a["xT"])
        ln_steps = moments, variance, lambda t: normalized(t).then_inc(a["xn"], 1)
        moments(0)
        variance(0)
        for i in range(2):
            dve.memset(V[i][:, :, :], 0.0).then_inc(v_made, 1)
            dve.memset(vprev[i][:, :, :], 0.0).then_inc(v_made, 1)
            dve.memset(qo[i][0:64, :, :].bitcast(F32), 0.0).then_inc(v_made, 1)
        dve.wait_ge(made, 3)
        dve.wait_ge(v_made, 6)
        ln_steps[2](0)

        def self_attention(i, par, on, starts=0):
            keys = self_qkv[:, 1, :].rearrange("p (c n) -> p c n", c=4)
            for u in range(8):
                w = u - 2
                n, is_on, _ = unit(i, par, on, w)
                if is_on and w % 2 == 0:
                    dve.wait_ge(a["tr"], n + 1)
                    dve.wait_ge(a["pv"], n - 1)
                    dve.tensor_copy(pt[0][:, :, :], self_t[:, 0, 0:3 * P].rearrange("p (a n) -> p a n", a=3)).then_inc(a["ev0"], 1)
                if on[1] and u == 0:
                    dve.wait_ge(a["S"], C + (i - 1) * 8)
                    dve.tensor_copy(before_of(kst[par])[:, 4:8], twice(keys[:, :, P - W:P])).then_inc(a["pD"], 1)
                if on[0] and u == 1:
                    dve.wait_ge(a["xh"], C + i + 1)
                    less_high(xtl[:, :, :], self_qkv[:, 0, 0:D].rearrange("p (c n) -> p c n", c=DC), xth[:, :, :]).then_inc(a["xl"], 1)
                if on[2] and u == 3:
                    dve.wait_ge(a["pv"], C + (i - 1) * 8)
                    dve.wait_ge(a["rS"], C + i - 1)
                    dve.tensor_tensor(o_sb[:, :, :], self_o, o_sb[:, :, :], ALU.mult).then_inc(a["on"], 1)
                if on[2] and u == 4:
                    dve.wait_ge(a["oh"], C + i - 1)
                    less_high(otl[:, :, :], o_sb[:, :, :], oth[:, :, :]).then_inc(a["ol"], 1)
                if on[0] and u == 3:
                    dve.wait_ge(a["qkv"], C + i + 1)
                    dve.wait_ge(a["pv"], C + i * 8 - 8)
                    dve.wait_ge(a_vp[1 - par], (i + par) * 16 + C)
                    dve.tensor_copy(V[par][:, :, 0:DH], self_qkv[:, 1, 0:D].rearrange("p (h d) -> p h d", h=H)).then_inc(a["v"], 1)
                    dve.wait_ge(a["hi"], C + i + 1)
                    dve.scalar_tensor_tensor(qs[:, :, 32:48], self_qkv[:, 0, 0:D].rearrange("p (h d) -> p h d", h=H), DH ** -0.5,
                                             qs[:, :, 0:16], ALU.mult, ALU.subtract)
                    less_high(ks[:, :, 16:32], self_qkv[:, 0, D:2 * D].rearrange("p (h d) -> p h d", h=H), ks[:, :, 0:16]).then_inc(a["lo"], 1)
                if starts and not par and u == 5:
                    dve.wait_ge(a["pA"], C + i)
                    dve.wait_ge(a["pD"], C + i)
                    dve.tensor_copy(before_of(kst[0]), twice(kinit[:, :, :])).then_inc(a_k0, 1)
                if on[3] and 4 <= u < 7:
                    ln_steps[u - 4](i + 1)
                if on[0] and u == 5:
                    dve.wait_ge(a["qT"], C + i + 1)
                    dve.tensor_copy(qo[par][64:P, :, :].rearrange("p (a c) n -> p a (c n)", a=2), self_qkv[64:P, :, :]).then_inc(a["qO"], 1)
                if on[1]:
                    n, _, _ = unit(i, par, on, u)
                    dve.wait_ge(a["S"], n + 1)
                    dve.tensor_reduce(negm[:, 1 - par, 2 * u:2 * u + 2], self_s[:, u % 2, 0:2 * KW].rearrange("p (n k) -> p n k", n=2),
                                      AX.X, ALU.max, negate=True).then_inc(a["max"], 1)
                if on[2] and u == 0:
                    dve.wait_ge(a["exp"], C + (i - 1) * 8)
                    dve.wait_ge(a["rT"], C + i - 2)
                    dve.reciprocal(den[:, par, :], den[:, par, :]).then_inc(a["rc"], 1)
                    dve.wait_ge(a["rc"], C + i - 1)
                    dve.tensor_copy(rden[:, :, :], den[:, par, :].unsqueeze(2).broadcast_to([P, H, HROW])).then_inc(a["rd"], 1)
                if on[2] and u == 6:
                    dve.wait_ge(a["op"], C + i - 1)
                    xt = tile_of(i - 2)
                    dve.tensor_tensor(xt, self_m[:, 0:D], xt, ALU.add).then_inc(a["x1"], 1)
                if on[0] and u == 7:
                    dve.wait_ge(a["kT"], C + i + 1)
                    dve.tensor_copy(kst[par][:, 4:8, W:KW], keys).then_inc(a["kD"], 1)

        dve.tensor_copy(before_of(kst[0]), twice(kinit[:, :, :])).then_inc(a_k0, 1)
        sweep_self_attention(dve, self_attention)

        dve.wait_ge(a["x1"], C + NT)
        dve.wait_ge(ld["small"], 48)

        def cross(i, par, on):
            if on[3]:
                t = i - 3
                dve.wait_ge(c["o"], C + t + 1)
                dve.wait_ge(c["bo"], C + t + 1)
                xt = tile_of(t)
                dve.tensor_tensor(xt, cross_o, xt, ALU.add).then_inc(c["x2"], 1)
                dve.wait_ge(c["x2"], C + t + 1)
                moments3(t)
                variance3(t)
            if on[0]:
                moments(i)
                variance(i)
            if on[3]:
                normalized3(t).then_inc(c["xn3"], 1)
            if on[0]:
                normalized(i).then_inc(c["xn"], 1)
            if on[3]:
                dve.wait_ge(c["xn3"], C + t + 1)
                dve.tensor_copy(XN3[:, bass.ds(t, 1), :].rearrange("p t d -> p (t d)"), XN3c[:, :]).then_inc(c["x3c"], 1)
            if on[1]:
                dve.wait_ge(c["exp"], C + (i - 1) * 2)
                for k, (ps, h0, h1) in enumerate(BANKS):
                    dve.wait_ge(c["S"], C + (i - 1) * 3 + k + 1)
                    dve.tensor_reduce(negm2[:, h0:h1], ps[:, 0:(h1 - h0) * CK].rearrange("p (h k) -> p h k", k=CK),
                                      AX.X, ALU.max, negate=True).then_inc(c["max"], 1)
                dve.wait_ge(c["max"], C + i * 3)
                dve.wait_ge(c["pT"], C + (i - 2) * 3)
                for ps, h0, h1 in BANKS[1:]:
                    dve.tensor_tensor(prob2[1 - par][:, h0:h1, :], ps[:, 0:(h1 - h0) * CK].rearrange("p (h k) -> p h k", k=CK),
                                      negm2[:, h0:h1].unsqueeze(2).broadcast_to([P, h1 - h0, CK]), ALU.add).then_inc(c["sub"], 1)
            if on[0]:
                dve.wait_ge(c["xh"], C + i + 1)
                less_high(xt2l[:, :, :], cross_x.rearrange("p (c n) -> p c n", c=DC), xt2h[:, :, :]).then_inc(c["xl"], 1)
            if on[2]:
                for k, (c0, c1) in enumerate(TCH):
                    dve.wait_ge(c["ph"], C + (i - 2) * 3 + k + 1)
                    if k < 2:
                        last = less_high(ptl[:, c0:c1, :], cross_t[k].rearrange("p (a n) -> p a n", a=4), pth[:, c0:c1, :])
                    else:
                        less_high(ptl[:, c0, :], cross_t[k][:, 0:P], pth[:, c0, :])
                        last = less_high(ptl[0:FLAST, c0 + 1, :], cross_t[k][0:FLAST, P:2 * P], pth[0:FLAST, c0 + 1, :])
                    last.then_inc(c["pl"], 1)
            if on[1]:
                dve.wait_ge(c["nrm"], C + i - 2)
                dve.wait_ge(c["exp"], C + i * 2)
                h1 = BANKS[0][2]
                dve.tensor_reduce(den2[:, 0, h1:XH], prob2[1 - par][:, h1:XH, :], AX.X, ALU.add).then_inc(c["sum"], 1)
                dve.wait_ge(c["sum"], C + i)
                dve.reciprocal(den2[:, 1, :], den2[:, 0, :]).then_inc(c["rd"], 1)
            if on[3]:
                dve.wait_ge(c["lg"], C + i - 2)
                dve.tensor_copy(logits[:, bass.ds(i - 3, 1), :].rearrange("p t e -> p (t e)"), cross_l).then_inc(c["lgc"], 1)

        moments, variance, normalized = layer_norm_steps(xn2[:, :], tile_of, stats2, c["ln"], c["xT"])
        moments3, variance3, normalized3 = layer_norm_steps(XN3c[:, :], tile_of, stats3, c["ln3"], c["x3T"])
        sweep(dve, 0, NT // 2, cross, 4)

        done = 0

        def route(ins):
            nonlocal done
            done += 1
            ins.then_inc(rt, 1)
            dve.wait_ge(rt, done)

        def over_experts(m):
            return m.unsqueeze(2).broadcast_to([P, NT, E])

        shifted, expd, hot0, hot1, sel_, dest8 = (m[:, :, :] for m in e8)
        peak, total, rtotal = (m[:, :] for m in s16[0:3])
        dve.wait_ge(c["lgc"], C + NT)
        route(dve.tensor_reduce(peak, logits[:, :, :], AX.X, ALU.max))
        route(dve.tensor_tensor(shifted, logits[:, :, :], over_experts(peak), ALU.subtract))
        assert done == RT_SHIFTED
        dve.wait_ge(rt_act, 1)
        route(dve.tensor_reduce(total, expd, AX.X, ALU.add))
        route(dve.reciprocal(rtotal, total))
        route(dve.tensor_tensor(shifted, expd, over_experts(rtotal), ALU.mult))
        for t in range(NT):
            last = dve.max(best[:, t, :], shifted[:, t, :])
        route(last)
        for t in range(NT):
            last = dve.max_index(besti[:, t, :], best[:, t, :], shifted[:, t, :])
        route(last)
        route(dve.tensor_copy(bestf[:, :, :], besti[:, :, 0:2]))
        dve.wait_ge(rt_idx, 2)
        every = iota8[:, :].unsqueeze(1).broadcast_to([P, NT, E])
        dve.tensor_tensor(hot0, every, bestf[:, :, 0:1].broadcast_to([P, NT, E]), ALU.is_equal)
        route(dve.tensor_tensor(hot1, every, bestf[:, :, 1:2].broadcast_to([P, NT, E]), ALU.is_equal))
        route(dve.tensor_tensor(sel_, hot0, hot1, ALU.add))
        assert done == RT_SEL
        dve.wait_ge(rt_pe, 2)
        tot3 = total_ps.rearrange("p (t e) -> p t e", e=E)
        dve.tensor_copy(run[0][:, :, :], tot3)
        dve.tensor_copy(run0, tot3)
        route(dve.tensor_copy(dest8, rank_ps.rearrange("p (t e) -> p t e", e=E)))

        end = None

        def slots_of_pairs():
            nonlocal end
            src, span = 0, 1
            while span < NT:
                dve.tensor_copy(run[1 - src][:, 0:span, :], run[src][:, 0:span, :])
                route(dve.tensor_tensor(run[1 - src][:, span:NT, :], run[src][:, span:NT, :], run[src][:, 0:NT - span, :], ALU.add))
                src, span = 1 - src, span * 2
            count = run[src][:, NT - 1, :]
            route(dve.tensor_scalar(counts[0][:, :], count, float(P - 1), None, ALU.add))
            route(dve.tensor_copy(countsi[0][:, :], counts[0][:, :]))
            route(dve.tensor_scalar(countsi[1][:, :], countsi[0][:, :], P.bit_length() - 1, None, ALU.arith_shift_right))
            route(dve.tensor_copy(counts[3][:, :], countsi[1][:, :]))
            route(dve.tensor_scalar(counts[3][:, :], counts[3][:, :], 1.0, None, ALU.max))
            route(dve.tensor_copy(counts[0][:, :], counts[3][:, :]))
            at, span = 0, 1
            while span < E:
                dve.tensor_copy(counts[1 - at][:, 0:span], counts[at][:, 0:span])
                route(dve.tensor_tensor(counts[1 - at][:, span:E], counts[at][:, span:E], counts[at][:, 0:E - span], ALU.add))
                at, span = 1 - at, span * 2
            end, first = counts[at][:, :], counts[2][:, :]
            route(dve.tensor_tensor(first, end, counts[3][:, :], ALU.subtract))
            route(dve.tensor_scalar(first, first, float(P), None, ALU.mult))
            route(dve.tensor_tensor(run0, run[src][:, :, :], run0, ALU.subtract))
            route(dve.tensor_tensor(dest8, run0, dest8, ALU.add))
            route(dve.tensor_tensor(dest8, dest8, first.unsqueeze(1).broadcast_to([P, NT, E]), ALU.add))
            for k, hot in enumerate((hot0, hot1)):
                route(dve.tensor_tensor(hot, hot, dest8, ALU.mult))
                route(dve.tensor_reduce(destf[:, k, :], hot, AX.X, ALU.add))
            route(dve.tensor_copy(dest[:, :, :], destf[:, :, :]))

        def tables():
            route(dve.tensor_tensor(total, best[:, :, 0], best[:, :, 1], ALU.add))
            route(dve.tensor_scalar(total, total, 1e-9, None, ALU.add))
            route(dve.reciprocal(rtotal, total))
            route(dve.tensor_tensor(gate[:, :, :], best[:, :, 0:2], rtotal.unsqueeze(2).broadcast_to([P, NT, 2]), ALU.mult))
            route(dve.tensor_tensor(owner8[:, :, :], iotab[:, :].unsqueeze(2).broadcast_to([1, BLOCKS, E]),
                                    end[0:1, :].unsqueeze(1).broadcast_to([1, BLOCKS, E]), ALU.is_ge))
            route(dve.tensor_reduce(owner[0][:, :], owner8[:, :, :], AX.X, ALU.add))
            route(dve.tensor_scalar(owner[0][:, :], owner[0][:, :], float(E - 1), 1.0, ALU.min, ALU.add))
            route(dve.tensor_copy(stage_of[:, :], owner[0][:, :]))
            assert PLACES == 3 and all(g * 11 // 32 == g // 3 for g in range(E + 1))
            route(dve.tensor_scalar(owner[1][:, :], owner[0][:, :], 11.0, None, ALU.mult))
            route(dve.tensor_copy(place_of[:, :], owner[1][:, :]))
            route(dve.tensor_scalar(place_of[:, :], place_of[:, :], 5, None, ALU.arith_shift_right))
            route(dve.tensor_copy(owner[1][:, :], place_of[:, :]))
            route(dve.scalar_tensor_tensor(owner[1][:, :], owner[1][:, :], -3.0, owner[0][:, :], ALU.mult, ALU.add))
            route(dve.tensor_copy(place_of[:, :], owner[1][:, :]))
            route(dve.tensor_copy(ends[0:1, 0:E], end[0:1, :]))
            route(dve.tensor_scalar(owner[1][0:1, 0:1], end[0:1, E - 1:E], 1.0, None, ALU.add))
            route(dve.tensor_copy(ends[0:1, E:E + 1], owner[1][0:1, 0:1]))
            route(dve.tensor_scalar(pairs_i[:, :], ends[0:1, E:E + 1], 1, None, ALU.arith_shift_right))
            dve.tensor_copy(ends[0:1, E:E + 1], pairs_i[:, :]).then_inc(rt_done, 1)

        def experts(routed):
            def body(i, par, on):
                if on[0]:
                    dve.wait_ge(f["xh"], C + i + 1)
                    less_high(fxl[:, :, :], ffn_x.rearrange("p (c n) -> p c n", c=DC), fxh[:, :, :]).then_inc(f["xl"], 1)
                if on[2] and not routed:
                    dve.wait_ge(f["dn"], C + i - 1)
                    xt = tile_of(i - 2)
                    dve.tensor_tensor(xt, down_y, xt, ALU.add).then_inc(f["y"], 1)
                if on[1]:
                    for n in range(2):
                        dve.wait_ge(f["hh"], C + (i - 1) * 2 + n + 1)
                        less_high(htl[:, 4 * n:4 * n + 4, :], down_t[:, n, :].rearrange("p (a n) -> p a n", a=4),
                                  hth[:, 4 * n:4 * n + 4, :]).then_inc(f["hl"], 1)
            return body

        sweep(dve, 0, NT // 2, experts(False), beside=(slots_of_pairs, tables))
        dve.wait_ge(rt_done, 1)
        pairs = dve.value_load(ends[0:1, E:E + 1], min_val=NT, max_val=BLOCKS // 2)
        sweep(dve, NT, pairs, experts(True))
        for t in range(NT):
            dve.wait_ge(g_y[t], 32)
            dve.scalar_tensor_tensor(X[:, t, :], ya[:, t, :], gate[:, t, 0:1], X[:, t, :], ALU.mult, ALU.add).then_inc(g_add, 1)
            dve.wait_ge(g_add, 2 * t + 1)
            dve.scalar_tensor_tensor(X[:, t, :], yb[:, t, :], gate[:, t, 1:2], X[:, t, :], ALU.mult, ALU.add).then_inc(g_add, 1)

    block_ctx.__exit__(None, None, None)


_INS = ['x', 'ctx_768', 'L0_attn_Wq', 'L0_attn_Wk', 'L0_attn_Wv', 'L0_attn_Wo', 'L0_attn_last_k_init',
        'L0_attn_last_v_init', 'L0_xattn_w_q', 'L0_xattn_w_k', 'L0_xattn_w_v', 'L0_xattn_w_out',
        'L0_xattn_b_out', 'L0_ffn_shared_w1', 'L0_ffn_shared_b1', 'L0_ffn_shared_w2', 'L0_ffn_shared_b2',
        'L0_ffn_router_w', 'L0_ffn_router_b', 'L0_ffn_exp_w1', 'L0_ffn_exp_b1', 'L0_ffn_exp_w2',
        'L0_ffn_exp_b2']
_OUTS = [((2, 1024, 256), 'float32')]


def kernel(**inputs):
    import numpy as _np
    import concourse.bacc as _bacc
    from concourse import mybir as _mybir
    from concourse.bass_utils import run_bass_kernel_spmd as _run

    nc = _bacc.Bacc("TRN2", target_bir_lowering=False, num_devices=1)
    arrays, args = {}, []
    for name in _INS:
        a = _np.ascontiguousarray(inputs[name])
        arrays[f"in_{name}_dram"] = a
        args.append(nc.dram_tensor(f"in_{name}_dram", a.shape, _mybir.dt.from_np(a.dtype), kind="ExternalInput").ap())
    for i, (shape, dtype) in enumerate(_OUTS):
        dt = _mybir.dt.from_np(_np.dtype(dtype))
        args.append(nc.dram_tensor(f"out_{i}_dram", shape, dt, kind="ExternalOutput").ap())
    decoder_layer(nc, *args)
    r = _run(nc, [arrays], core_ids=[0])
    return r.results[0]["out_0_dram"]
```
